# Optimizing a Trainium2 kernel written in Bass

```python
import numpy as np
import jax
import jax.numpy as jnp

def _softmax(x, axis=-1):
    return jax.nn.softmax(x, axis=axis)

def _gelu(x):
    return jax.nn.gelu(x, approximate=True)

def _silu(x):
    return jax.nn.silu(x)

def _sigmoid(x):
    return jax.nn.sigmoid(x)

def _layernorm(x, axis=-1, eps=1e-05):
    m = jnp.mean(x, axis=axis, keepdims=True)
    v = jnp.var(x, axis=axis, keepdims=True)
    return (x - m) / jnp.sqrt(v + eps)

def _scatter_add(tgt, idx, src, axis=0):
    return tgt.at[idx].add(src)

def _segment_sum(src, seg, n):
    return jax.ops.segment_sum(src, seg, n)
kernel_name = 'mk_vit_tower_postln_d2_tok_img1024_r4_964632'

def setup_inputs(seed: int=0):
    np.random.seed(seed)
    _w = jnp.asarray

    def _rec_inputs():
        import jax
        import jax.numpy as jnp
        _rk = jax.random.key(seed)
        x = -7.10856e-05 + 0.999911 * jax.random.normal(jax.random.fold_in(_rk, 1), (4, 512, 256, 4), jnp.float32)
        return x
    x = _rec_inputs()

    def _L0_tok_setup():
        import jax, jax.numpy as jnp
        import numpy as np
        B, S, D, E = (8, 512, 256, 4)
        DE = 512
        key = jax.random.key(seed)
        k1, k2, k3, k4 = jax.random.split(key, 4)
        scale = 1.0 / np.sqrt(D)
        return {'expert_id': 0, 'freq_features': jax.random.normal(k1, (B, S, D, E), dtype=jnp.float32), 'W0': jax.random.normal(k2, (DE, D), dtype=jnp.float32) * scale, 'W1': jax.random.normal(k3, (DE, D), dtype=jnp.float32) * scale, 'Wo': jax.random.normal(k4, (D, DE), dtype=jnp.float32) * (1.0 / np.sqrt(DE))}
    _L0_tok_all = _L0_tok_setup()
    _L0_tok_in = {k: v for k, v in _L0_tok_all.items() if k in ('W0', 'W1', 'Wo')}
    del _L0_tok_all

    def _L0_attn_setup():
        import jax, jax.numpy as jnp
        import numpy as np
        import math
        EMBED_DIM = 256
        NUM_HEADS = 16
        HEAD_DIM = EMBED_DIM // NUM_HEADS
        WINDOW_SIZE = 128
        BATCH = 2
        SEQ_LEN = 512

        def _sliding_window_mask(seq_len: int, window_size: int) -> jnp.ndarray:
            i = jnp.arange(seq_len)[:, None]
            j = jnp.arange(seq_len)[None, :]
            allowed = jnp.abs(i - j) <= window_size // 2
            return jnp.where(allowed, 0.0, -jnp.inf).astype(jnp.float32)

        def _split_heads(t):
            b, s, d = t.shape
            return t.reshape(b, s, NUM_HEADS, HEAD_DIM).transpose(0, 2, 1, 3)
        key = jax.random.key(seed)
        ks = jax.random.split(key, 9)
        s = 1.0 / math.sqrt(EMBED_DIM)
        inp = {'x': jax.random.normal(ks[0], (BATCH, SEQ_LEN, EMBED_DIM), dtype=jnp.float32), 'Wq': jax.random.normal(ks[1], (EMBED_DIM, EMBED_DIM), dtype=jnp.float32) * s, 'bq': jnp.zeros((EMBED_DIM,), dtype=jnp.float32), 'Wk': jax.random.normal(ks[2], (EMBED_DIM, EMBED_DIM), dtype=jnp.float32) * s, 'bk': jnp.zeros((EMBED_DIM,), dtype=jnp.float32), 'Wv': jax.random.normal(ks[3], (EMBED_DIM, EMBED_DIM), dtype=jnp.float32) * s, 'bv': jnp.zeros((EMBED_DIM,), dtype=jnp.float32), 'Wo': jax.random.normal(ks[4], (EMBED_DIM, EMBED_DIM), dtype=jnp.float32) * s, 'bo': jnp.zeros((EMBED_DIM,), dtype=jnp.float32)}
        return inp
    _L0_attn_all = _L0_attn_setup()
    _L0_attn_in = {k: v for k, v in _L0_attn_all.items() if k in ('Wq', 'bq', 'Wk', 'bk', 'Wv', 'bv', 'Wo', 'bo')}
    del _L0_attn_all

    def _L0_ffn_setup():
        import jax, jax.numpy as jnp
        import numpy as np
        EPS = 1e-05

        def act_quant(x):
            scale = 127.0 / jnp.clip(jnp.max(jnp.abs(x), axis=-1, keepdims=True), EPS, None)
            q = jnp.clip(jnp.round(x * scale), -128.0, 127.0) / scale
            return x + jax.lax.stop_gradient(q - x)

        def weight_quant(w):
            scale = 1.0 / jnp.clip(jnp.mean(jnp.abs(w)), EPS, None)
            q = jnp.clip(jnp.round(w * scale), -1.0, 1.0) / scale
            return w + jax.lax.stop_gradient(q - w)

        def bitlinear(x, w):
            return act_quant(x) @ weight_quant(w).T
        key = jax.random.key(seed)
        k1, k2, k3, k4 = jax.random.split(key, 4)
        H, I = (256, 1024)
        B, S = (4, 1024)
        init = 0.02
        x = jax.random.normal(k1, (B, S, H), dtype=jnp.float32)
        w_gate = jax.random.normal(k2, (I, H), dtype=jnp.float32) * init
        w_up = jax.random.normal(k3, (I, H), dtype=jnp.float32) * init
        w_down = jax.random.normal(k4, (H, I), dtype=jnp.float32) * init
        return {'x': x, 'w_gate': w_gate, 'w_up': w_up, 'w_down': w_down}
    _L0_ffn_all = _L0_ffn_setup()
    _L0_ffn_in = {k: v for k, v in _L0_ffn_all.items() if k in ('w_gate', 'w_up', 'w_down')}
    del _L0_ffn_all

    def _L1_attn_setup():
        import jax, jax.numpy as jnp
        import numpy as np
        D_EMB = 256
        N_H = 16
        D_H = D_EMB // N_H
        key = jax.random.key(seed)
        ks = jax.random.split(key, 9)
        s = 1.0 / np.sqrt(D_EMB)
        inp = {'x': jax.random.normal(ks[0], (2, 512, D_EMB), dtype=jnp.float32)}
        for i, name in enumerate(['q', 'k', 'v', 'o']):
            inp[f'W{name}'] = jax.random.uniform(ks[1 + 2 * i], (D_EMB, D_EMB), minval=-s, maxval=s, dtype=jnp.float32)
            inp[f'b{name}'] = jax.random.uniform(ks[2 + 2 * i], (D_EMB,), minval=-s, maxval=s, dtype=jnp.float32)
        return inp
    _L1_attn_all = _L1_attn_setup()
    _L1_attn_in = {k: v for k, v in _L1_attn_all.items() if k in ('Wq', 'bq', 'Wk', 'bk', 'Wv', 'bv', 'Wo', 'bo')}
    del _L1_attn_all

    def _L1_ffn_setup():
        import jax, jax.numpy as jnp
        import numpy as np
        TOP_K = 2
        CAP_FACTOR = 1.25
        EPS = 1.1920929e-07
        key = jax.random.key(seed)
        ks = jax.random.split(key, 6)
        B, S, D, E, H = (8, 512, 256, 8, 1024)
        return {'hidden_states': jax.random.normal(ks[0], (B, S, D), jnp.float32), 'wg': jax.random.normal(ks[1], (D, E), jnp.float32) * 0.02, 'fc1_w': jax.random.normal(ks[2], (E, H, D), jnp.float32) * 0.02, 'fc1_b': jnp.zeros((E, H), jnp.float32), 'fc2_w': jax.random.normal(ks[3], (E, H, D), jnp.float32) * 0.02, 'fc2_b': jnp.zeros((E, D), jnp.float32), 'ln_gamma': jnp.ones((D,), jnp.float32), 'ln_beta': jnp.zeros((D,), jnp.float32)}
    _L1_ffn_all = _L1_ffn_setup()
    _L1_ffn_in = {k: v for k, v in _L1_ffn_all.items() if k in ('wg', 'fc1_w', 'fc1_b', 'fc2_w', 'fc2_b', 'ln_gamma', 'ln_beta')}
    del _L1_ffn_all
    return {'x': x, 'L0_tok_W0': _L0_tok_in['W0'], 'L0_tok_W1': _L0_tok_in['W1'], 'L0_tok_Wo': _L0_tok_in['Wo'], 'L0_attn_Wq': _L0_attn_in['Wq'], 'L0_attn_bq': _L0_attn_in['bq'], 'L0_attn_Wk': _L0_attn_in['Wk'], 'L0_attn_bk': _L0_attn_in['bk'], 'L0_attn_Wv': _L0_attn_in['Wv'], 'L0_attn_bv': _L0_attn_in['bv'], 'L0_attn_Wo': _L0_attn_in['Wo'], 'L0_attn_bo': _L0_attn_in['bo'], 'L0_ffn_w_gate': _L0_ffn_in['w_gate'], 'L0_ffn_w_up': _L0_ffn_in['w_up'], 'L0_ffn_w_down': _L0_ffn_in['w_down'], 'L1_attn_Wq': _L1_attn_in['Wq'], 'L1_attn_bq': _L1_attn_in['bq'], 'L1_attn_Wk': _L1_attn_in['Wk'], 'L1_attn_bk': _L1_attn_in['bk'], 'L1_attn_Wv': _L1_attn_in['Wv'], 'L1_attn_bv': _L1_attn_in['bv'], 'L1_attn_Wo': _L1_attn_in['Wo'], 'L1_attn_bo': _L1_attn_in['bo'], 'L1_ffn_wg': _L1_ffn_in['wg'], 'L1_ffn_fc1_w': _L1_ffn_in['fc1_w'], 'L1_ffn_fc1_b': _L1_ffn_in['fc1_b'], 'L1_ffn_fc2_w': _L1_ffn_in['fc2_w'], 'L1_ffn_fc2_b': _L1_ffn_in['fc2_b'], 'L1_ffn_ln_gamma': _L1_ffn_in['ln_gamma'], 'L1_ffn_ln_beta': _L1_ffn_in['ln_beta']}

def reference(x, L0_tok_W0, L0_tok_W1, L0_tok_Wo, L0_attn_Wq, L0_attn_bq, L0_attn_Wk, L0_attn_bk, L0_attn_Wv, L0_attn_bv, L0_attn_Wo, L0_attn_bo, L0_ffn_w_gate, L0_ffn_w_up, L0_ffn_w_down, L1_attn_Wq, L1_attn_bq, L1_attn_Wk, L1_attn_bk, L1_attn_Wv, L1_attn_bv, L1_attn_Wo, L1_attn_bo, L1_ffn_wg, L1_ffn_fc1_w, L1_ffn_fc1_b, L1_ffn_fc2_w, L1_ffn_fc2_b, L1_ffn_ln_gamma, L1_ffn_ln_beta):
    import jax
    import jax.numpy as jnp

    def _L0_tok_ref(expert_id, freq_features, W0, W1, Wo):
        import jax, jax.numpy as jnp
        import numpy as np
        B, S, D, E = (8, 512, 256, 4)
        DE = 512
        x = freq_features[:, :, :, expert_id]
        gate = jax.nn.relu(jnp.einsum('bsd,ed->bse', x, W0))
        up = jnp.einsum('bsd,ed->bse', x, W1)
        hidden = gate * up
        out = jnp.einsum('bse,de->bsd', hidden, Wo)
        return out

    def _L0_attn_ref(x, Wq, bq, Wk, bk, Wv, bv, Wo, bo):
        import jax, jax.numpy as jnp
        import numpy as np
        import math
        EMBED_DIM = 256
        NUM_HEADS = 16
        HEAD_DIM = EMBED_DIM // NUM_HEADS
        WINDOW_SIZE = 128
        BATCH = 2
        SEQ_LEN = 512

        def _sliding_window_mask(seq_len: int, window_size: int) -> jnp.ndarray:
            i = jnp.arange(seq_len)[:, None]
            j = jnp.arange(seq_len)[None, :]
            allowed = jnp.abs(i - j) <= window_size // 2
            return jnp.where(allowed, 0.0, -jnp.inf).astype(jnp.float32)

        def _split_heads(t):
            b, s, d = t.shape
            return t.reshape(b, s, NUM_HEADS, HEAD_DIM).transpose(0, 2, 1, 3)
        b, s, d = x.shape
        q = _split_heads(x @ Wq + bq)
        k = _split_heads(x @ Wk + bk)
        v = _split_heads(x @ Wv + bv)
        scores = jnp.einsum('bhqd,bhkd->bhqk', q, k) / math.sqrt(HEAD_DIM)
        scores = scores + _sliding_window_mask(s, WINDOW_SIZE)
        probs = jax.nn.softmax(scores, axis=-1)
        attn = jnp.einsum('bhqk,bhkd->bhqd', probs, v)
        attn = attn.transpose(0, 2, 1, 3).reshape(b, s, d)
        return attn @ Wo + bo

    def _L0_ffn_ref(x, w_gate, w_up, w_down):
        import jax, jax.numpy as jnp
        import numpy as np
        EPS = 1e-05

        def act_quant(x):
            scale = 127.0 / jnp.clip(jnp.max(jnp.abs(x), axis=-1, keepdims=True), EPS, None)
            q = jnp.clip(jnp.round(x * scale), -128.0, 127.0) / scale
            return x + jax.lax.stop_gradient(q - x)

        def weight_quant(w):
            scale = 1.0 / jnp.clip(jnp.mean(jnp.abs(w)), EPS, None)
            q = jnp.clip(jnp.round(w * scale), -1.0, 1.0) / scale
            return w + jax.lax.stop_gradient(q - w)

        def bitlinear(x, w):
            return act_quant(x) @ weight_quant(w).T
        g = bitlinear(x, w_gate)
        u = bitlinear(x, w_up)
        h = jnp.square(jax.nn.relu(g)) * u
        return bitlinear(h, w_down)

    def _L1_attn_ref(x, Wq, bq, Wk, bk, Wv, bv, Wo, bo):
        import jax, jax.numpy as jnp
        import numpy as np
        D_EMB = 256
        N_H = 16
        D_H = D_EMB // N_H
        B, S, D = x.shape
        Q = x @ Wq.T + bq
        K = x @ Wk.T + bk
        V = x @ Wv.T + bv
        Qh = Q.reshape(B, S, N_H, D_H).transpose(0, 2, 1, 3)
        Kh = K.reshape(B, S, N_H, D_H).transpose(0, 2, 1, 3)
        Vh = V.reshape(B, S, N_H, D_H).transpose(0, 2, 1, 3)
        scores = jnp.einsum('bhsd,bhtd->bhst', Qh, Kh) / jnp.sqrt(jnp.float32(D_H))
        causal = jnp.tril(jnp.ones((S, S), dtype=bool))
        scores = jnp.where(causal, scores, -jnp.inf)
        attn = jax.nn.softmax(scores, axis=-1)
        out = jnp.einsum('bhst,bhtd->bhsd', attn, Vh)
        out = out.transpose(0, 2, 1, 3).reshape(B, S, D)
        return out @ Wo.T + bo

    def _L1_ffn_ref(hidden_states, wg, fc1_w, fc1_b, fc2_w, fc2_b, ln_gamma, ln_beta):
        import jax, jax.numpy as jnp
        import numpy as np
        TOP_K = 2
        CAP_FACTOR = 1.25
        EPS = 1.1920929e-07
        B, S, D = hidden_states.shape
        E = wg.shape[1]
        N = B * S
        k = TOP_K
        C = k * int(CAP_FACTOR * ((N + E - 1) // E))
        x = hidden_states.reshape(N, D)
        scores = jax.nn.softmax(x @ wg, axis=-1)
        gates, idx = jax.lax.top_k(scores, k)
        gates = gates / jnp.clip(jnp.sum(gates, -1, keepdims=True), EPS)
        masks = jax.nn.one_hot(idx, E, dtype=jnp.int32)
        counts = masks.sum(0)
        offsets = jnp.concatenate([jnp.zeros((1, E), jnp.int32), jnp.cumsum(counts, 0)[:-1]], 0)
        loc = jnp.cumsum(masks, 0) - 1 + offsets[None]
        loc_sel = (loc * masks).sum(-1)
        keep = loc_sel < C
        gates = gates * keep.astype(gates.dtype)
        pos = jnp.where(keep, idx * C + loc_sel, E * C)
        xk = jnp.broadcast_to(x[:, None, :], (N, k, D)).reshape(N * k, D)
        buf = jnp.zeros((E * C + 1, D), x.dtype).at[pos.reshape(-1)].set(xk)
        disp = buf[:E * C].reshape(E, C, D)
        h = jax.nn.silu(jnp.einsum('ecd,ehd->ech', disp, fc1_w) + fc1_b[:, None, :])
        y = jnp.einsum('ech,ehd->ecd', h, fc2_w) + fc2_b[:, None, :]
        ybuf = jnp.concatenate([y.reshape(E * C, D), jnp.zeros((1, D), y.dtype)], 0)
        combined = jnp.sum(gates[..., None] * ybuf[pos], axis=1)
        res = hidden_states + combined.reshape(B, S, D)
        mu = jnp.mean(res, -1, keepdims=True)
        var = jnp.var(res, -1, keepdims=True)
        return (res - mu) * jax.lax.rsqrt(var + 1e-05) * ln_gamma + ln_beta
    h = _L0_tok_ref(0, x, L0_tok_W0, L0_tok_W1, L0_tok_Wo)
    h = _layernorm(h + _L0_attn_ref(h, L0_attn_Wq, L0_attn_bq, L0_attn_Wk, L0_attn_bk, L0_attn_Wv, L0_attn_bv, L0_attn_Wo, L0_attn_bo), axis=-1)
    h = _layernorm(h + _L0_ffn_ref(h, L0_ffn_w_gate, L0_ffn_w_up, L0_ffn_w_down), axis=-1)
    h = _layernorm(h + _L1_attn_ref(h, L1_attn_Wq, L1_attn_bq, L1_attn_Wk, L1_attn_bk, L1_attn_Wv, L1_attn_bv, L1_attn_Wo, L1_attn_bo), axis=-1)
    h = _layernorm(h + _L1_ffn_ref(h, L1_ffn_wg, L1_ffn_fc1_w, L1_ffn_fc1_b, L1_ffn_fc2_w, L1_ffn_fc2_b, L1_ffn_ln_gamma, L1_ffn_ln_beta), axis=-1)
    return h

_drawn_inputs = setup_inputs


def setup_inputs(seed=0):
    import zlib

    import numpy as np

    out = dict(_drawn_inputs(seed))
    spreads = {'L0_attn_bq': (0.0, 0.732),
     'L0_attn_bk': (0.0, 0.8),
     'L0_attn_bv': (0.0, 0.1),
     'L0_attn_bo': (0.0, 0.1),
     'L1_ffn_fc1_b': (0.0, 0.694),
     'L1_ffn_fc2_b': (0.0, 0.1),
     'L1_ffn_ln_gamma': (1.0, 0.2),
     'L1_ffn_ln_beta': (0.0, 0.1)}
    factors = {'L0_ffn_w_gate': 8.0,
     'L0_ffn_w_up': 8.0,
     'L0_ffn_w_down': 8.0,
     'L1_attn_Wq': 3.963,
     'L1_attn_bq': 8.0,
     'L1_attn_Wk': 3.867,
     'L1_attn_bk': 8.0}
    for name, (base, spread) in spreads.items():
        noise = np.random.default_rng([zlib.crc32(name.encode()), seed]).standard_normal(out[name].shape)
        drawn = base * np.exp(spread * noise) if base else spread * noise
        out[name] = jnp.asarray(drawn.astype(out[name].dtype))
    for name, factor in factors.items():
        out[name] = (out[name] * factor).astype(out[name].dtype)
    return out
```

```python
from contextlib import ExitStack

import concourse.bass as bass
import numpy as np
from concourse import mybir

F32 = mybir.dt.float32
BF16 = mybir.dt.bfloat16
U32 = mybir.dt.uint32
ALU = mybir.AluOpType
ACT = mybir.ActivationFunctionType
AX = mybir.AxisListType

P = 128
B, S, D = 4, 512, 256
N = B * S
KD = D // P
NT = S // P
NTT = N // P
DE = 512
ME = DE // P
H, DH = 16, 16
SLOT = 32
HG = P // SLOT
NG = H // HG
AUG = DH
HALF_WINDOW = 64
I0 = 1024
MI = I0 // P
E, HE = 8, 1024
MH = HE // P
CAP = 2 * int(1.25 * ((N + E - 1) // E))
CT = CAP // P
ROWS = E * CAP
HC = CAP // 2
EPS_LN = 1e-5
EPS_Q = 1e-5
EPS_GATE = 1.1920929e-07
MAGIC = 1.5 * 2.0 ** 23
MASKED = -1.0e30

C_ID, C_CM, C_WM, C_TRI, C_ONE, C_REV, C_IDX, C_END = 0, 128, 640, 896, 1024, 1152, 1280, 1408
WINDOW, CAUSAL = 0, 1


def q_range(kind, kt):
    if kind == CAUSAL:
        return kt * P, S
    return max(0, kt * P - HALF_WINDOW), min(S, (kt + 1) * P + HALF_WINDOW)


def k_range(kind, t):
    if kind == CAUSAL:
        return 0, (t + 1) * P
    return max(0, t * P - HALF_WINDOW), min(S, (t + 1) * P + HALF_WINDOW)


def build(nc, xT, w01, wtok, wattn, wo, battn, brow, wq0, wdn, wgate, consts, w1, w2, b1, b2, lnrow, out):
    disp = nc.dram_tensor("dispatched_rows", (ROWS, D), F32, kind="Internal").ap()
    ydram = nc.dram_tensor("expert_rows", (ROWS + P, D), F32, kind="Internal").ap()
    ctx = ExitStack()
    with ctx:
        def sb(name, shape, dt=F32):
            return ctx.enter_context(nc.sbuf_tensor(name, shape, dt))

        def sem(name):
            return ctx.enter_context(nc.semaphore(name))

        cst = sb("cst", [P, C_END])
        identb = sb("identb", [P, P], BF16)
        trib = sb("trib", [P, 2 * P], BF16)
        tokw = sb("tokw", [P, KD, 2 * DE])
        tokwo = sb("tokwo", [P, ME, D])
        aw = [sb(f"aw{l}", [P, KD, 2 * NG * P + D]) for l in range(2)]
        awo = [sb(f"awo{l}", [P, KD, D]) for l in range(2)]
        ab = [sb(f"ab{l}", [P, 2 * NG]) for l in range(2)]
        ar = [sb(f"ar{l}", [P, 2 * D]) for l in range(2)]
        qgu = sb("qgu", [P, KD, 2 * I0], BF16)
        qdn = sb("qdn", [P, MI, D], BF16)
        gatew = sb("gatew", [P, KD, E])
        h3 = sb("h3", [P, NTT, D])
        logits = sb("logits", [P, NTT, E])
        x_sb = sb("x_sb", [P, KD, N])
        h = sb("h", [P, NT, D])
        res = sb("res", [P, NT, D])
        hT = sb("hT", [P, KD, S])
        att = sb("att", [P, NT, D])
        attT = sb("attT", [P, KD, S])
        lnx = sb("lnx", [P, NT, D])
        stat = sb("stat", [P, 4, 6])
        mv = sb("mv", [P, NTT, 2])
        rstd = sb("rstd", [P, NTT, 2])
        small = sb("small", [P, 32])
        wsc = sb("wsc", [P, 16])
        neg_half = sb("neg_half", [P, 4])

        ident = cst[:, C_ID:C_ID + P]
        ones = cst[:, C_ONE:C_ONE + P]

        ps = ctx.enter_context(nc.psum_tensor("ps", [P, 8, 512], F32))

        def bank(i):
            return ps[:, i, :]

        for_x, for_tok, for_attn, for_ffn, for_cst = (sem(n) for n in (
            "for_x", "for_tok", "for_attn", "for_ffn", "for_cst"))
        prep = sem("prep")
        prep_act = sem("prep_act")
        prep_pe = sem("prep_pe")
        prep_pool = sem("prep_pool")
        zeroed = sem("zeroed")
        routed = sem("routed")
        route_pe = sem("route_pe")
        route_act = sem("route_act")
        dve_route = sem("dve_route")
        scattered = sem("scattered")
        gathered = sem("gathered")
        stored = sem("stored")
        wa_in = sem("wa_in")
        go = [sem(f"go{i}") for i in range(3)]

        arrived = sem("arrived")
        bs = {n: sem(n) for n in (
            "gu_mm", "relu_done", "hid_done", "h0_mm", "h0_done",
            "hT_mm0", "hT_done0", "hT_mm1", "hT_done1", "hT_mm2", "hT_done2",
            "fq_done", "fq_mm", "fqT_done", "fgu_mm", "fsq_done", "fh_done", "fq2_done", "fq2_mm", "fq2T_done",
            "fdn_mm", "lg_mm", "lg_done", "keep_done", "dve_chain", "act_chain", "pool_chain")}
        for l in range(2):
            for n in ("qk_mm", "q_done", "k_done", "v_mm", "v_done", "s_mm", "max_done", "nm_mm", "qa_done",
                      "st_mm", "exp_done", "sel_done", "pv_mm", "ot_done", "ob_mm", "o_done", "oT_mm", "oT_done",
                      "pr_mm", "res_done"):
                bs[f"{n}{l}"] = sem(f"{n}{l}")
        for l in range(3):
            for n in ("lns_done", "var_done", "rstd_done", "ln_done"):
                bs[f"{n}{l}"] = sem(f"{n}{l}")
        batch_range = range(arrived.num, max(s.num for s in bs.values()) + 1)
        assert len(batch_range) == len(bs) + 1

        e_arrived = sem("e_arrived")
        es = {n: sem(n) for n in ("wb_in", "xT_mm", "xT_done", "f1_mm", "silu_done", "f2_mm", "y_done", "y_out",
                                  "wa_next")}
        expert_range = range(e_arrived.num, max(s.num for s in es.values()) + 1)
        assert len(expert_range) == len(es) + 1

        c_arrived = sem("c_arrived")
        cs = {n: sem(n) for n in ("mix_done", "cvar_done", "crstd_done", "cn_done", "out_done", "c_chain",
                                  "fin_done")}
        combine_range = range(c_arrived.num, max(s.num for s in cs.values()) + 1)
        assert len(combine_range) == len(cs) + 1

        def turn_ends(eng, gate, turn, counter, clear=None):
            if clear is not None:
                eng.wait_ge(counter, 4)
                eng.sem_clear(clear)
                eng.sem_inc(gate, 1)
            else:
                eng.sem_inc(counter, 1)
                eng.wait_ge(gate, turn + 1)

        with ExitStack() as c2:
            def sb2(name, shape, dt=F32):
                return c2.enter_context(nc.sbuf_tensor(name, shape, dt))

            relu_g = sb2("relu_g", [P, 2, DE])
            hid = sb2("hid", [P, ME, S])
            qT = sb2("qT", [P, NG, S])
            kT = sb2("kT", [P, NG, S])
            vaug = sb2("vaug", [P, NT, H * SLOT])
            nmp = sb2("nmp", [P, 2, NT, P])
            junk = sb2("junk", [P, 2, S])
            probs = sb2("probs", [P, 3, HG, S])
            oT = sb2("oT", [P, NG, S])
            rsum = sb2("rsum", [P, NT, H])
            fq = sb2("fq", [P, D])
            fqb = sb2("fqb", [P, 2, D], BF16)
            fqT = sb2("fqT", [P, 2, KD, P], BF16)
            fr = hid[:, 0:2, :].rearrange("p a n -> p (a n)")
            fsq = hid[:, 2:4, :].rearrange("p a n -> p (a n)")
            fh = sb2("fh", [P, I0])
            fq2 = sb2("fq2", [P, I0], BF16)
            fq2T = sb2("fq2T", [P, MI, P], BF16)
            zero_rows = sb2("zero_rows", [P, 2, D])
            wgu_f = [qT[:, :, :].rearrange("p g s -> p (g s)"), kT[:, :, :].rearrange("p g s -> p (g s)")]
            wdn_f = oT[:, :, :].rearrange("p g s -> p (g s)")

            with nc.Block() as block:
                @block.sync
                def _(sp):
                    for k in range(KD):
                        sp.dma_start(tokw[:, k, :], w01[:, k, :]).then_inc(for_tok, 16)
                        for b in range(2):
                            sp.dma_start(x_sb[:, k, b * 2 * S:(b + 1) * 2 * S],
                                         xT[0, k * P:(k + 1) * P, b * 2 * S:(b + 1) * 2 * S]).then_inc(for_x, 16)
                    sp.dma_start(tokwo[:, :, :], wtok).then_inc(for_tok, 16)
                    for n in range(2):
                        sp.dma_start(wgu_f[n], wq0[n]).then_inc(for_ffn, 16)
                    sp.dma_start(wdn_f, wdn).then_inc(for_ffn, 16)
                    sp.wait_ge(prep_pool, 1)
                    for c in range(ROWS // (2 * P)):
                        sp.dma_start(disp[c * 2 * P:(c + 1) * 2 * P, :].rearrange("(p r) d -> p r d", r=2),
                                     zero_rows[:, :, :]).then_inc(zeroed, 16)
                    sp.dma_start(ydram[ROWS:ROWS + P, :], zero_rows[:, 0, :]).then_inc(zeroed, 16)
                    with sp.Fori(0, B) as b:
                        turn_ends(sp, go[0], b, arrived, clear=batch_range)
                    sp.wait_ge(zeroed, 16 * (ROWS // (2 * P) + 1))

                @block.gpsimd
                def _(pool):
                    pool.memset(zero_rows[:, :, :], 0.0).then_inc(prep_pool, 1)
                    pool.memset(neg_half[:, :], -0.5)
                    pool.memset(nmp[:, :, :, :], 0.0)
                    pool.memset(vaug[:, :, :], 0.0).then_inc(prep_pool, 1)
                    pool.wait_ge(prep_pool, 2)
                    pool.memset(vaug[:, :, :].rearrange("p t (h s) -> p (t h) s", s=SLOT)[:, :, DH:DH + 1],
                                1.0).then_inc(prep_pool, 1)

                    def residual(l, ready, count):
                        for t in range(NT):
                            if ready is not None:
                                pool.wait_ge(bs[ready], count + t)
                            pool.tensor_tensor(res[:, t, :], h[:, t, :], ar[l][:, D:2 * D],
                                               ALU.add).then_inc(bs[f"res_done{l}"], 1)

                    def select(kind, l):
                        for u in range(NG * NT):
                            kt = u % NT
                            lo, hi = q_range(kind, kt)
                            pool.wait_ge(bs[f"exp_done{l}"], 2 * u + 2)
                            cuts = []
                            if kind == CAUSAL:
                                cuts.append((0, P, 0, 1, -1))
                            else:
                                cut = kt * P + HALF_WINDOW - lo
                                cuts.append((0, cut, lo - kt * P + HALF_WINDOW, 1, -1))
                                cuts.append((cut, hi - lo, 0, -1, 1))
                            for i, (a, z, base, step, mult) in enumerate(cuts):
                                part = probs[:, u % 3, :, a:z]
                                ins = pool.affine_select(out=part, in_=part, compare_op=ALU.is_ge, fill=0.0,
                                                         base=base, pattern=[[0, HG], [step, z - a]],
                                                         channel_multiplier=mult)
                            ins.then_inc(bs[f"sel_done{l}"], 1)

                    def rstds(n, rows):
                        for t in range(rows):
                            pool.wait_ge(bs[f"var_done{n}"], t + 1)
                            pool.tensor_tensor(rstd[:, t, 0:1], mv[:, t, 1:2], neg_half[:, 0:1],
                                               ALU.pow).then_inc(bs[f"rstd_done{n}"], 1)

                    with pool.Fori(0, B) as b:
                        pool.wait_ge(for_attn, 16 * 8)
                        residual(0, "h0_done", 1)
                        select(WINDOW, 0)
                        rstds(0, NT)
                        rstds(1, NT)
                        residual(1, "ln_done1", 1)
                        select(CAUSAL, 1)
                        rstds(2, NT)
                        pool.wait_ge(bs["ln_done2"], NT)
                        pool.tensor_copy(h3[:, bass.ds(b * NT, NT), :], h[:, :, :]).then_inc(bs["keep_done"], 1)
                        pool.wait_ge(bs["keep_done"], 1)
                        turn_ends(pool, go[0], b, arrived)

                @block.scalar
                def _(act):
                    act.dma_start(cst[:, :], consts).then_inc(for_cst, 16)
                    for l in range(2):
                        act.dma_start(aw[l][:, :, :], wattn[l]).then_inc(for_attn, 16)
                        act.dma_start(awo[l][:, :, :], wo[l]).then_inc(for_attn, 16)
                        act.dma_start(ab[l][:, :], battn[l]).then_inc(for_attn, 16)
                        act.dma_start(ar[l][:, :], brow[l]).then_inc(for_attn, 16)
                    act.dma_start(gatew[:, :, :], wgate).then_inc(for_cst, 16)

                    def turned(n, l):
                        for t in range(NT):
                            act.wait_ge(bs[f"hT_mm{n}"], t + 1)
                            act.activation(hT[:, :, t * P:(t + 1) * P],
                                           bank(6 + t % 2)[:, 0:KD * P].rearrange("p (k n) -> p k n", k=KD),
                                           ACT.Copy).then_inc(bs[f"hT_done{n}"], 1)

                    def attention(kind, l):
                        for g in range(NG):
                            act.wait_ge(bs[f"qk_mm{l}"], 2 * g + 2)
                            act.activation(kT[:, g, :], bank((2 * g + 1) % 4), ACT.Identity,
                                           bias=ab[l][:, NG + g:NG + g + 1]).then_inc(bs[f"k_done{l}"], 1)
                        for u in range(NG * NT):
                            g, kt = divmod(u, NT)
                            lo, hi = q_range(kind, kt)
                            if u >= 3:
                                act.wait_ge(bs[f"pv_mm{l}"], u - 2)
                            for half in range(2):
                                v = 2 * u + half
                                pair = 2 * (1 - half)
                                act.wait_ge(bs[f"st_mm{l}"], v + 1)
                                act.activation(probs[:, u % 3, pair:pair + 2, 0:hi - lo],
                                               ps[:, 2 * (v % 2):2 * (v % 2) + 2, 0:hi - lo],
                                               ACT.Exp).then_inc(bs[f"exp_done{l}"], 1)
                            if kt == 0 and g:
                                act.wait_ge(bs[f"pv_mm{l}"], NT * g)
                                act.activation(oT[:, g - 1, :], bank(6), ACT.Copy).then_inc(bs[f"ot_done{l}"], 1)
                        act.wait_ge(bs[f"pv_mm{l}"], NT * NG)
                        act.activation(oT[:, NG - 1, :], bank(6), ACT.Copy).then_inc(bs[f"ot_done{l}"], 1)
                        for t in range(NT):
                            act.wait_ge(bs[f"oT_mm{l}"], t + 1)
                            act.activation(attT[:, :, t * P:(t + 1) * P],
                                           bank(6 + t % 2)[:, 0:KD * P].rearrange("p (k n) -> p k n", k=KD),
                                           ACT.Copy).then_inc(bs[f"oT_done{l}"], 1)

                    with act.Fori(0, B) as b:
                        for m in range(ME):
                            act.wait_ge(bs["gu_mm"], m + 1)
                            if m >= 2:
                                act.wait_ge(bs["hid_done"], m - 1)
                            act.activation(relu_g[:, m % 2, :], bank(2 * (m % 2)),
                                           ACT.Relu).then_inc(bs["relu_done"], 1)
                        turned(0, 0)
                        act.wait_ge(for_attn, 16 * 8)
                        attention(WINDOW, 0)
                        for t in range(NT):
                            act.wait_ge(bs["fq_mm"], t + 1)
                            if t >= 2:
                                act.wait_ge(bs["fgu_mm"], t - 1)
                            act.activation(fqT[:, t % 2, :, :],
                                           bank(6 + t % 2).bitcast(BF16)[:, 0:KD * P].rearrange(
                                               "p (k n) -> p k n", k=KD), ACT.Copy).then_inc(bs["fqT_done"], 1)
                            act.wait_ge(bs["fgu_mm"], t + 1)
                            act.activation(hid[:, 0:2, :], ps[:, 0:2, :],
                                           ACT.Relu).then_inc(bs["act_chain"], 1)
                            act.wait_ge(bs["act_chain"], t + 1)
                            if t:
                                act.wait_ge(bs["fh_done"], t)
                            act.activation(fsq, fr, ACT.Square).then_inc(bs["fsq_done"], 1)
                            act.wait_ge(bs["fq2_mm"], t + 1)
                            if t:
                                act.wait_ge(bs["fdn_mm"], t)
                            act.activation(fq2T[:, :, :],
                                           bank(4).bitcast(BF16).rearrange("p (k n) -> p k n", k=MI),
                                           ACT.Copy).then_inc(bs["fq2T_done"], 1)
                        turned(1, 0)
                        attention(CAUSAL, 1)
                        turned(2, 0)
                        act.wait_ge(bs["hT_done2"], NT)
                        turn_ends(act, go[0], b, arrived)

                @block.tensor
                def _(pe):
                    mm = pe.matmul

                    def turn(n, ready):
                        def one(t):
                            pe.wait_ge(bs[ready], t + 1)
                            if t >= 2:
                                pe.wait_ge(bs[f"hT_done{n}"], t - 1)
                            for k in range(KD):
                                ins = pe.transpose(bank(6 + t % 2)[:, k * P:(k + 1) * P],
                                                   h[:, t, k * P:(k + 1) * P], ident)
                            ins.then_inc(bs[f"hT_mm{n}"], 1)
                        return one

                    def attention(kind, l, hT_ready):
                        w = aw[l]
                        pe.wait_ge(bs[hT_ready], NT)
                        for i in range(2 * NG):
                            g, is_k = divmod(i, 2)
                            if g >= 2:
                                pe.wait_ge(bs[f"{'k' if is_k else 'q'}_done{l}"], g - 1)
                            c = (is_k * NG + g) * P
                            for k in range(KD):
                                ins = mm(bank(i % 4), w[:, k, c:c + P], hT[:, k, :], start=(k == 0),
                                         stop=(k == KD - 1))
                            ins.then_inc(bs[f"qk_mm{l}"], 1)
                        for t in range(NT):
                            if t >= 2:
                                pe.wait_ge(bs[f"v_done{l}"], t - 1)
                            for k in range(KD):
                                ins = mm(bank(4 + t % 2)[:, 0:D], hT[:, k, t * P:(t + 1) * P],
                                         w[:, k, 2 * NG * P:], start=(k == 0), stop=(k == KD - 1))
                            ins.then_inc(bs[f"v_mm{l}"], 1)
                        pe.wait_ge(bs[f"v_done{l}"], NT)

                        def scores(g, t, pair):
                            if t == 0 and pair == 0:
                                pe.wait_ge(bs[f"q_done{l}"], g + 1)
                                pe.wait_ge(bs[f"k_done{l}"], g + 1)
                            lo, hi = k_range(kind, t)
                            for j in (pair, pair + 1):
                                i = g * NT * HG + t * HG + j
                                if i >= 2:
                                    pe.wait_ge(bs[f"max_done{l}"], i - 1)
                                r = slice(SLOT * j, SLOT * j + SLOT)
                                mm(bank(4 + j % 2)[:, 0:hi - lo], qT[r, g, t * P:(t + 1) * P], kT[r, g, lo:hi],
                                   start=True, stop=True, tile_position=(SLOT * j, 0)).then_inc(bs[f"s_mm{l}"], 1)

                        def maxima(g):
                            pe.wait_ge(bs[f"max_done{l}"], NT * HG * (g + 1))
                            if g:
                                pe.wait_ge(bs[f"qa_done{l}"], g)
                            for t in range(NT):
                                ins = pe.transpose(bank(7)[:, t * P:(t + 1) * P], nmp[:, g % 2, t, :], ident)
                            ins.then_inc(bs[f"nm_mm{l}"], 1)

                        def scores_T(g, kt, half):
                            u = g * NT + kt
                            v = 2 * u + half
                            pair = 2 * (1 - half)
                            lo, hi = q_range(kind, kt)
                            if kt == 0 and half == 0:
                                pe.wait_ge(bs[f"qa_done{l}"], g + 1)
                            if v >= 2:
                                pe.wait_ge(bs[f"exp_done{l}"], v - 1)
                            else:
                                pe.wait_ge(bs[f"k_done{l}"], NG)
                                pe.wait_ge(bs[f"q_done{l}"], NG)
                            for i in range(2):
                                j = pair + i
                                r = slice(SLOT * j, SLOT * j + SLOT)
                                ins = mm(bank(2 * (v % 2) + i)[:, 0:hi - lo], kT[r, g, kt * P:(kt + 1) * P],
                                         qT[r, g, lo:hi], start=True, stop=True, tile_position=(SLOT * j, 0))
                            ins.then_inc(bs[f"st_mm{l}"], 1)

                        def values(g, kt):
                            u = g * NT + kt
                            lo, hi = q_range(kind, kt)
                            pe.wait_ge(bs[f"sel_done{l}"], u + 1)
                            if kt == 0 and g:
                                pe.wait_ge(bs[f"ot_done{l}"], g)
                            for j in range(HG):
                                hd = g * HG + j
                                ins = mm(bank(6)[SLOT * j:SLOT * j + SLOT, lo:hi],
                                         vaug[:, kt, hd * SLOT:(hd + 1) * SLOT], probs[:, u % 3, j, 0:hi - lo],
                                         start=(kt == 0), stop=(kt == NT - 1), skip_group_check=True,
                                         tile_position=(0, SLOT * j))
                            ins.then_inc(bs[f"pv_mm{l}"], 1)

                        late = []
                        for g in range(NG + 1):
                            for t in range(NT):
                                for half in range(2):
                                    if g < NG:
                                        scores(g, t, 2 * half)
                                    if g and t == 0 and half == 0:
                                        maxima(g - 1)
                                    if g:
                                        scores_T(g - 1, t, half)
                                        if half == 0 and late:
                                            values(*late.pop(0))
                                if g:
                                    late.append((g - 1, t))
                        values(*late.pop(0))

                        def heads_back(t):
                            if t == 0:
                                pe.wait_ge(bs[f"ot_done{l}"], NG)
                            if t >= 2:
                                pe.wait_ge(bs[f"o_done{l}"], t - 1)
                            for g in range(NG):
                                ins = pe.transpose(bank(4 + t % 2)[:, g * P:(g + 1) * P],
                                                   oT[:, g, t * P:(t + 1) * P], ident)
                            ins.then_inc(bs[f"ob_mm{l}"], 1)

                        def heads_turn(t):
                            pe.wait_ge(bs[f"o_done{l}"], t + 1)
                            if t >= 2:
                                pe.wait_ge(bs[f"oT_done{l}"], t - 1)
                            for k in range(KD):
                                ins = pe.transpose(bank(6 + t % 2)[:, k * P:(k + 1) * P],
                                                   att[:, t, k * P:(k + 1) * P], ident)
                            ins.then_inc(bs[f"oT_mm{l}"], 1)

                        def project(t):
                            pe.wait_ge(bs[f"oT_done{l}"], t + 1)
                            if t >= 2:
                                pe.wait_ge(bs[f"lns_done{2 * l}"], t - 1)
                            for k in range(KD):
                                ins = mm(bank(t % 2)[:, 0:D], attT[:, k, t * P:(t + 1) * P], awo[l][:, k, :],
                                         start=(k == 0), stop=(k == KD - 1))
                            ins.then_inc(bs[f"pr_mm{l}"], 1)

                        for s in range(NT + 2):
                            if s < NT:
                                heads_back(s)
                            if 1 <= s < NT + 1:
                                heads_turn(s - 1)
                            if s >= 2:
                                project(s - 2)

                    pe.wait_ge(prep, 1)
                    mm(bank(7)[:, 0:4], ones, wsc[:, 0:4], start=True, stop=True).then_inc(prep_pe, 1)
                    pe.wait_ge(for_x, 16 * 4)
                    pe.wait_ge(for_tok, 16 * 3)
                    pe.wait_ge(for_cst, 16 * 2)
                    pe.wait_ge(prep_pool, 3)
                    pe.wait_ge(prep, 2)
                    with pe.Fori(0, B) as b:
                        for m in range(ME):
                            if m >= 2:
                                pe.wait_ge(bs["hid_done"], m - 1)
                            for n in range(2):
                                c = n * DE + m * P
                                for k in range(KD):
                                    ins = mm(bank(2 * (m % 2) + n), tokw[:, k, c:c + P], x_sb[:, k, bass.ds(b * S, S)],
                                             start=(k == 0), stop=(k == KD - 1))
                            ins.then_inc(bs["gu_mm"], 1)
                        turn0 = turn(0, "h0_done")
                        pe.wait_ge(bs["hid_done"], ME)
                        for t in range(NT + 1):
                            if t < NT:
                                if t >= 2:
                                    pe.wait_ge(bs["h0_done"], t - 1)
                                for m in range(ME):
                                    ins = mm(bank(4 + t % 2)[:, 0:D], hid[:, m, t * P:(t + 1) * P], tokwo[:, m, :],
                                             start=(m == 0), stop=(m == ME - 1))
                                ins.then_inc(bs["h0_mm"], 1)
                            if t:
                                turn0(t - 1)
                        pe.wait_ge(for_attn, 16 * 8)
                        attention(WINDOW, 0, "hT_done0")

                        def f_turn(t):
                            pe.wait_ge(bs["fq_done"], t + 1)
                            if t >= 2:
                                pe.wait_ge(bs["fqT_done"], t - 1)
                            for k in range(KD):
                                ins = pe.transpose(bank(6 + t % 2).bitcast(BF16)[:, k * P:(k + 1) * P],
                                                   fqb[:, t % 2, k * P:(k + 1) * P], identb[:, :])
                            ins.then_inc(bs["fq_mm"], 1)

                        def f_up(t):
                            pe.wait_ge(bs["fqT_done"], t + 1)
                            if t:
                                pe.wait_ge(bs["fh_done"], t)
                            else:
                                pe.wait_ge(bs["lns_done0"], NT)
                            for n in range(4):
                                for k in range(KD):
                                    ins = mm(bank(n), fqT[:, t % 2, k, :], qgu[:, k, n * 512:(n + 1) * 512],
                                             start=(k == 0), stop=(k == KD - 1))
                            ins.then_inc(bs["fgu_mm"], 1)

                        def f_turn2(t):
                            pe.wait_ge(bs["fq2_done"], t + 1)
                            if t:
                                pe.wait_ge(bs["fq2T_done"], t)
                            for k in range(MI):
                                ins = pe.transpose(bank(4).bitcast(BF16)[:, k * P:(k + 1) * P],
                                                   fq2[:, k * P:(k + 1) * P], identb[:, :])
                            ins.then_inc(bs["fq2_mm"], 1)

                        def f_down(t):
                            pe.wait_ge(bs["fq2T_done"], t + 1)
                            if t:
                                pe.wait_ge(bs["lns_done1"], t)
                            for k in range(MI):
                                ins = mm(bank(5)[:, 0:D], fq2T[:, k, :], qdn[:, k, :], start=(k == 0),
                                         stop=(k == MI - 1))
                            ins.then_inc(bs["fdn_mm"], 1)

                        turn1 = turn(1, "ln_done1")
                        f_turn(0)
                        f_up(0)
                        for t in range(NT):
                            if t + 1 < NT:
                                f_turn(t + 1)
                            f_turn2(t)
                            if t + 1 < NT:
                                f_up(t + 1)
                            f_down(t)
                        for t in range(NT):
                            turn1(t)
                        attention(CAUSAL, 1, "hT_done1")
                        turn2 = turn(2, "ln_done2")
                        for t in range(NT):
                            turn2(t)
                        pe.wait_ge(bs["hT_done2"], NT)
                        for t in range(NT):
                            for k in range(KD):
                                ins = mm(bank(4)[:, t * E:(t + 1) * E], hT[:, k, t * P:(t + 1) * P], gatew[:, k, :],
                                         start=(k == 0), stop=(k == KD - 1))
                        ins.then_inc(bs["lg_mm"], 1)
                        pe.wait_ge(bs["lg_mm"], 1)
                        turn_ends(pe, go[0], b, arrived)

                @block.vector
                def _(dve):
                    done = [0]

                    def link(ins):
                        done[0] += 1
                        ins.then_inc(bs["dve_chain"], 1)
                        dve.wait_ge(bs["dve_chain"], done[0])

                    dve.wait_ge(for_ffn, 16 * 3)
                    dve.wait_ge(for_cst, 32)
                    dve.wait_ge(prep_pool, 3)
                    link(dve.memset(wsc[:, :], 0.0))
                    ws = (wgu_f[0], wgu_f[1], wdn_f)
                    for n, w in enumerate(ws):
                        ins = dve.tensor_reduce(wsc[:, n:n + 1], w, AX.X, ALU.add, apply_absolute_value=True)
                    ins.then_inc(prep, 1)
                    dve.tensor_copy(identb[:, :], ident)
                    dve.tensor_copy(trib[:, :], cst[:, C_TRI:C_TRI + 2 * P])
                    dve.wait_ge(prep_pe, 1)
                    link(dve.tensor_scalar(wsc[:, 4:8], bank(7)[:, 0:4], 1.0 / (I0 * D), EPS_Q, ALU.mult, ALU.max))
                    link(dve.reciprocal(wsc[:, 8:12], wsc[:, 4:8]))
                    for n, w in enumerate(ws):
                        q = qgu[:, :, n * I0:(n + 1) * I0] if n < 2 else qdn[:, :, :]
                        link(dve.tensor_scalar(w, w, wsc[:, 8 + n:9 + n], MAGIC, ALU.mult, ALU.add))
                        link(dve.tensor_scalar(w, w, MAGIC + 1.0, MAGIC - 1.0, ALU.min, ALU.max))
                        link(dve.tensor_scalar(q, w.rearrange("p (k n) -> p k n", k=q.shape[1]), MAGIC, None,
                                               ALU.subtract))
                    link(dve.tensor_tensor(wsc[:, 12:13], wsc[:, 4:5], wsc[:, 4:5], ALU.mult))
                    link(dve.tensor_tensor(wsc[:, 12:13], wsc[:, 12:13], wsc[:, 5:6], ALU.mult))
                    link(dve.tensor_scalar(wsc[:, 13:14], wsc[:, 6:7], 1.0 / 127.0, None, ALU.mult))
                    dve.nop().then_inc(prep, 1)
                    dve.sem_clear(bs["dve_chain"])
                    done[0] = 0

                    def ln_sum(n, t, psum, res_in, scale=None):
                        o = lnx[:, t, :]
                        if scale is None:
                            ins = dve.tensor_tensor(o, psum, res_in, ALU.add)
                        else:
                            ins = dve.scalar_tensor_tensor(o, psum, scale, res_in, ALU.mult, ALU.add)
                        ins.then_inc(bs[f"lns_done{n}"], 1)
                        dve.wait_ge(bs[f"lns_done{n}"], t + 1)
                        link(dve.bn_stats(stat[:, t % 2, :], o))
                        link(dve.bn_aggr(mv[:, t, :], stat[:, t % 2, :]))
                        dve.tensor_scalar(mv[:, t, 1:2], mv[:, t, 1:2], EPS_LN, None,
                                          ALU.add).then_inc(bs[f"var_done{n}"], 1)

                    def ln_out(n, t):
                        dve.wait_ge(bs[f"rstd_done{n}"], t + 1)
                        dve.tensor_scalar(h[:, t, :], lnx[:, t, :], mv[:, t, 0:1], rstd[:, t, 0:1], ALU.subtract,
                                          ALU.mult).then_inc(bs[f"ln_done{n}"], 1)

                    def attention(kind, l):
                        for g in range(NG):
                            dve.wait_ge(bs[f"qk_mm{l}"], 2 * g + 1)
                            dve.tensor_scalar(qT[:, g, :], bank((2 * g) % 4), ab[l][:, g:g + 1], DH ** -0.5, ALU.add,
                                              ALU.mult).then_inc(bs[f"q_done{l}"], 1)
                        for t in range(NT):
                            dve.wait_ge(bs[f"v_mm{l}"], t + 1)
                            dve.tensor_tensor(vaug[:, t, :].rearrange("p (h s) -> p h s", s=SLOT)[:, :, 0:DH],
                                              bank(4 + t % 2)[:, 0:D].rearrange("p (h s) -> p h s", s=DH),
                                              ar[l][:, 0:D].rearrange("p (h s) -> p h s", s=DH),
                                              ALU.add).then_inc(bs[f"v_done{l}"], 1)
                        for g in range(NG):
                            for t in range(NT):
                                lo, hi = k_range(kind, t)
                                if kind == CAUSAL:
                                    mask = cst[:, C_CM + S - (hi - lo):C_CM + S]
                                else:
                                    c = C_WM + lo - (t * P - HALF_WINDOW)
                                    mask = cst[:, c:c + hi - lo]
                                for j in range(HG):
                                    i = g * NT * HG + t * HG + j
                                    dve.wait_ge(bs[f"s_mm{l}"], i + 1)
                                    dve.tensor_tensor_reduce(
                                        out=junk[:, j % 2, 0:hi - lo], in0=bank(4 + j % 2)[:, 0:hi - lo], in1=mask,
                                        scale=-1.0, scalar=3.0e38, op0=ALU.add, op1=ALU.min,
                                        accum_out=nmp[:, g % 2, t, SLOT * j + AUG:SLOT * j + AUG + 1]
                                    ).then_inc(bs[f"max_done{l}"], 1)
                                    if g and t == 0 and j == 1:
                                        augment(l, g - 1)
                        augment(l, NG - 1)
                        for t in range(NT):
                            heads = bank(4 + t % 2).rearrange("p (h s) -> p h s", s=SLOT)
                            dve.wait_ge(bs[f"ob_mm{l}"], t + 1)
                            link(dve.reciprocal(rsum[:, t, :].rearrange("p (h o) -> p h o", o=1),
                                                heads[:, :, DH:DH + 1]))
                            dve.tensor_tensor(att[:, t, :].rearrange("p (h s) -> p h s", s=DH), heads[:, :, 0:DH],
                                              rsum[:, t, :].rearrange("p (h o) -> p h o", o=1).to_broadcast(
                                                  [P, H, DH]), ALU.mult).then_inc(bs[f"o_done{l}"], 1)
                        dve.wait_ge(bs[f"res_done{l}"], NT)
                        for t in range(NT + 1):
                            if t < NT:
                                dve.wait_ge(bs[f"pr_mm{l}"], t + 1)
                                ln_sum(2 * l, t, bank(t % 2)[:, 0:D], res[:, t, :])
                            if t:
                                ln_out(2 * l, t - 1)

                    def augment(l, g):
                        dve.wait_ge(bs[f"nm_mm{l}"], g + 1)
                        dve.tensor_tensor(qT[:, g, :], qT[:, g, :], bank(7), ALU.add).then_inc(bs[f"qa_done{l}"], 1)

                    def quant(t):
                        c = small[:, 8 * (t % 4):8 * (t % 4) + 8]
                        dve.wait_ge(bs["ln_done0"], t + 1)
                        link(dve.tensor_reduce(c[:, 0:1], h[:, t, :], AX.X, ALU.max, apply_absolute_value=True))
                        link(dve.tensor_scalar(c[:, 0:1], c[:, 0:1], EPS_Q, 1.0 / 127.0, ALU.max, ALU.mult))
                        link(dve.reciprocal(c[:, 1:2], c[:, 0:1]))
                        link(dve.tensor_scalar(fq[:, :], h[:, t, :], c[:, 1:2], MAGIC, ALU.mult, ALU.add))
                        if t >= 2:
                            dve.wait_ge(bs["fq_mm"], t - 1)
                        dve.tensor_scalar(fqb[:, t % 2, :], fq[:, :], MAGIC, 127.0, ALU.subtract,
                                          ALU.min).then_inc(bs["fq_done"], 1)
                        link(dve.tensor_tensor(c[:, 2:3], c[:, 0:1], c[:, 0:1], ALU.mult))
                        link(dve.tensor_tensor(c[:, 2:3], c[:, 2:3], c[:, 0:1], ALU.mult))
                        link(dve.tensor_tensor(c[:, 2:3], c[:, 2:3], wsc[:, 12:13], ALU.mult))

                    def hidden(t):
                        c = small[:, 8 * (t % 4):8 * (t % 4) + 8]
                        dve.wait_ge(bs["fsq_done"], t + 1)
                        dve.tensor_tensor(fh[:, :].rearrange("p (a n) -> p a n", a=2),
                                          hid[:, 2:4, :], ps[:, 2:4, :],
                                          ALU.mult).then_inc(bs["fh_done"], 1)
                        dve.wait_ge(bs["fh_done"], t + 1)
                        link(dve.tensor_reduce(c[:, 3:4], fh[:, :], AX.X, ALU.max, apply_absolute_value=True))
                        link(dve.tensor_tensor(c[:, 3:4], c[:, 3:4], c[:, 2:3], ALU.mult))
                        link(dve.tensor_scalar(c[:, 3:4], c[:, 3:4], EPS_Q, None, ALU.max))
                        link(dve.reciprocal(c[:, 4:5], c[:, 3:4]))
                        link(dve.tensor_tensor(c[:, 4:5], c[:, 4:5], c[:, 2:3], ALU.mult))
                        link(dve.tensor_scalar(c[:, 4:5], c[:, 4:5], 127.0, None, ALU.mult))
                        link(dve.tensor_tensor(c[:, 5:6], c[:, 3:4], wsc[:, 13:14], ALU.mult))
                        link(dve.tensor_scalar(fh[:, :], fh[:, :], c[:, 4:5], MAGIC, ALU.mult, ALU.add))
                        if t:
                            dve.wait_ge(bs["fq2_mm"], t)
                        dve.tensor_scalar(fq2[:, :], fh[:, :], MAGIC, 127.0, ALU.subtract,
                                          ALU.min).then_inc(bs["fq2_done"], 1)

                    with dve.Fori(0, B) as b:
                        for m in range(ME):
                            dve.wait_ge(bs["relu_done"], m + 1)
                            dve.tensor_tensor(hid[:, m, :], bank(2 * (m % 2) + 1), relu_g[:, m % 2, :],
                                              ALU.mult).then_inc(bs["hid_done"], 1)
                        for t in range(NT):
                            dve.wait_ge(bs["h0_mm"], t + 1)
                            dve.tensor_copy(h[:, t, :], bank(4 + t % 2)[:, 0:D]).then_inc(bs["h0_done"], 1)
                        dve.wait_ge(for_attn, 16 * 8)
                        attention(WINDOW, 0)
                        quant(0)
                        for t in range(NT):
                            if t + 1 < NT:
                                quant(t + 1)
                            hidden(t)
                            dve.wait_ge(bs["fdn_mm"], t + 1)
                            ln_sum(1, t, bank(5)[:, 0:D], h[:, t, :], scale=small[:, 8 * t + 5:8 * t + 6])
                            ln_out(1, t)
                        attention(CAUSAL, 1)
                        dve.wait_ge(bs["lg_mm"], 1)
                        dve.tensor_copy(logits[:, bass.ds(b * NT, NT), :],
                                        bank(4)[:, 0:NT * E].rearrange("p (t e) -> p t e", e=E)
                                        ).then_inc(bs["lg_done"], 1)
                        dve.wait_ge(bs["lg_done"], 1)
                        turn_ends(dve, go[0], b, arrived)
                        done[0] = 0

        with ExitStack() as c3:
            def sb3(name, shape, dt=F32):
                return c3.enter_context(nc.sbuf_tensor(name, shape, dt))

            R = {n: sb3(f"r_{n}", [P, NTT, E]) for n in ("e", "p", "q", "m0", "m1", "t0")}
            rc = sb3("rc", [P, 8, NTT])
            mk = sb3("mk", [P, 2, E, NTT], BF16)
            mkf = sb3("mkf", [P, 2, E, NTT])
            tot = sb3("tot", [P, 2, 2, E, NTT])
            exc = sb3("exc", [P, 2, E, NTT])
            loc = sb3("loc", [P, 2, NTT])
            idx = sb3("idx", [P, 2, NTT])
            keep = sb3("keep", [P, 2, NTT])
            gates = sb3("gates", [P, 2, NTT])
            posu = sb3("posu", [P, 2, NTT], U32)
            w1s = sb3("w1s", [P, 2, KD, HE])
            w2s = sb3("w2s", [P, 2, MH, D])
            b1s = sb3("b1s", [P, E, MH])
            b2s = sb3("b2s", [P, 2, D])
            lnr = sb3("lnr", [P, 2 * D])
            dx = sb3("dx", [P, 2, CT, D])
            dxT = sb3("dxT", [P, 2, KD, CAP])
            hTe = sb3("hTe", [P, MH, CAP])
            ysb = sb3("ysb", [P, CT, D])
            dx_v = disp.rearrange("(e t p) d -> e p t d", p=P, t=CT)
            y_v = ydram[0:ROWS, :].rearrange("(e t p) d -> e p t d", p=P, t=CT)

            with nc.Block() as block:
                def load_weights(eng, e, s, sem_):
                    eng.dma_start(w1s[:, s, :, :], w1[bass.ds(e, 1), :, :, :].rearrange("o p k n -> p (o k) n")
                                  ).then_inc(sem_, 16)
                    eng.dma_start(w2s[:, s, :, :], w2[bass.ds(e, 1), :, :, :].rearrange("o p k n -> p (o k) n")
                                  ).then_inc(sem_, 16)
                    eng.dma_start(b2s[:, s, :], b2[bass.ds(e, 1), :, :].rearrange("o p n -> p (o n)")
                                  ).then_inc(sem_, 16)

                def load_rows(eng, e, s, sem_):
                    eng.dma_start(dx[:, s, :, :], dx_v[bass.ds(e, 1), :, :, :].rearrange("o p t d -> p (o t) d")
                                  ).then_inc(sem_, 16)

                @block.sync
                def _(sp):
                    sp.dma_start(b1s[:, :, :], b1).then_inc(wa_in, 16)
                    sp.dma_start(lnr[:, :], lnrow).then_inc(wa_in, 16)
                    load_weights(sp, 0, 0, wa_in)
                    sp.wait_ge(scattered, 16 * 2 * NTT)
                    load_rows(sp, 0, 0, wa_in)
                    with sp.Fori(0, E // 2) as i:
                        load_weights(sp, i * 2 + 1, 1, es["wb_in"])
                        load_rows(sp, i * 2 + 1, 1, es["wb_in"])
                        nxt = (i * 2 + 2) % E
                        sp.wait_ge(es["f2_mm"], CT)
                        sp.wait_ge(es["y_done"], CT)
                        load_weights(sp, nxt, 0, es["wa_next"])
                        load_rows(sp, nxt, 0, es["wa_next"])
                        for j in range(2):
                            sp.wait_ge(es["y_done"], CT * (j + 1))
                            sp.dma_start(y_v[bass.ds(i * 2 + j, 1), :, :, :].rearrange("o p t d -> p (o t) d"),
                                         ysb[:, :, :]).then_inc(es["y_out"], 16)
                        sp.wait_ge(es["y_out"], 32)
                        sp.wait_ge(es["wa_next"], 64)
                        turn_ends(sp, go[1], i, e_arrived, clear=expert_range)

                @block.gpsimd
                def _(pool):
                    pool.wait_ge(routed, 1)
                    for t in range(NTT):
                        for k in range(2):
                            pool.indirect_dma_start(
                                out=disp, out_offset=bass.IndirectOffsetOnAxis(ap=posu[:, k, t:t + 1], axis=0),
                                in_=h3[:, t, :], in_offset=None, bounds_check=ROWS - 1,
                                oob_is_err=False).then_inc(scattered, 16)
                    with pool.Fori(0, E // 2) as i:
                        turn_ends(pool, go[1], i, e_arrived)

                @block.tensor
                def _(pe):
                    mm = pe.matmul
                    pe.wait_ge(route_pe, 1)
                    mf = mk[:, :, :, :].rearrange("p a b c -> p (a b c)")
                    mm(bank(0)[:, 0:2 * E * NTT], trib[:, 0:P], mf, start=True, stop=True)
                    mm(bank(1)[:, 0:2 * E * NTT], trib[:, P:2 * P], mf, start=True, stop=True).then_inc(route_pe, 1)
                    pe.wait_ge(wa_in, 16 * 6)

                    def turn_rows(s):
                        for t in range(CT):
                            n = s * CT + t
                            if n >= 2:
                                pe.wait_ge(es["xT_done"], n - 1)
                            for k in range(KD):
                                ins = pe.transpose(bank(6 + n % 2)[:, k * P:(k + 1) * P],
                                                   dx[:, s, t, k * P:(k + 1) * P], ident)
                            ins.then_inc(es["xT_mm"], 1)

                    def fc1(s):
                        pe.wait_ge(es["xT_done"], CT * (s + 1))
                        for m in range(MH):
                            n = s * MH + m
                            if n >= 2:
                                pe.wait_ge(es["silu_done"], n - 1)
                            for c in range(2):
                                for k in range(KD):
                                    ins = mm(bank(2 * (n % 2) + c)[:, 0:HC], w1s[:, s, k, m * P:(m + 1) * P],
                                             dxT[:, s, k, c * HC:(c + 1) * HC], start=(k == 0), stop=(k == KD - 1))
                            ins.then_inc(es["f1_mm"], 1)

                    def fc2(s):
                        pe.wait_ge(es["silu_done"], MH * (s + 1))
                        for t in range(CT):
                            n = s * CT + t
                            if n >= 2:
                                pe.wait_ge(es["y_done"], n - 1)
                            for m in range(MH):
                                ins = mm(bank(4 + n % 2)[:, 0:D], hTe[:, m, t * P:(t + 1) * P], w2s[:, s, m, :],
                                         start=(m == 0), stop=(m == MH - 1))
                            ins.then_inc(es["f2_mm"], 1)

                    with pe.Fori(0, E // 2) as i:
                        turn_rows(0)
                        fc1(0)
                        pe.wait_ge(es["wb_in"], 64)
                        turn_rows(1)
                        fc2(0)
                        fc1(1)
                        fc2(1)
                        pe.wait_ge(es["f2_mm"], 2 * CT)
                        turn_ends(pe, go[1], i, e_arrived)

                @block.scalar
                def _(act):
                    act.wait_ge(route_act, 1)
                    act.activation(R["e"][:, :, :], R["t0"][:, :, :], ACT.Exp).then_inc(route_act, 1)
                    act.wait_ge(wa_in, 16 * 6)
                    with act.Fori(0, E // 2) as i:
                        for s in range(2):
                            for m in range(MH):
                                n = s * MH + m
                                act.wait_ge(es["f1_mm"], n + 1)
                                if m == 0 and s:
                                    act.wait_ge(es["f2_mm"], CT)
                                act.activation(hTe[:, m, :].rearrange("p (a n) -> p a n", a=2),
                                               ps[:, 2 * (n % 2):2 * (n % 2) + 2, 0:HC], ACT.Silu,
                                               bias=b1s[:, bass.ds(i * 2 + s, 1), m:m + 1].rearrange(
                                                   "p a b -> p (a b)")).then_inc(es["silu_done"], 1)
                        act.wait_ge(es["silu_done"], 2 * MH)
                        turn_ends(act, go[1], i, e_arrived)

                @block.vector
                def _(dve):
                    done = [0]

                    def link(ins):
                        done[0] += 1
                        ins.then_inc(dve_route, 1)
                        dve.wait_ge(dve_route, done[0])

                    def bc(v):
                        return v.rearrange("p (t o) -> p t o", o=1).to_broadcast([P, NTT, E])

                    link(dve.tensor_reduce(rc[:, 0, :], logits[:, :, :], AX.X, ALU.max))
                    dve.tensor_tensor(R["t0"][:, :, :], logits[:, :, :], bc(rc[:, 0, :]),
                                      ALU.subtract).then_inc(route_act, 1)
                    dve.wait_ge(route_act, 2)
                    link(dve.tensor_reduce(rc[:, 1, :], R["e"][:, :, :], AX.X, ALU.add))
                    link(dve.reciprocal(rc[:, 2, :], rc[:, 1, :]))
                    link(dve.tensor_tensor(R["p"][:, :, :], R["e"][:, :, :], bc(rc[:, 2, :]), ALU.mult))
                    rev = cst[:, C_REV:C_REV + P].rearrange("p (t e) -> p t e", e=E)
                    ind = cst[:, C_IDX:C_IDX + P].rearrange("p (t e) -> p t e", e=E)
                    cur = R["p"]
                    for k in range(2):
                        link(dve.tensor_reduce(rc[:, 3 + k, :], cur[:, :, :], AX.X, ALU.max))
                        link(dve.tensor_tensor(R["t0"][:, :, :], cur[:, :, :], bc(rc[:, 3 + k, :]), ALU.is_equal))
                        link(dve.tensor_tensor(R["t0"][:, :, :], R["t0"][:, :, :], rev, ALU.mult))
                        link(dve.tensor_reduce(rc[:, 5, :], R["t0"][:, :, :], AX.X, ALU.max))
                        m = R[f"m{k}"]
                        link(dve.tensor_tensor(m[:, :, :], R["t0"][:, :, :], bc(rc[:, 5, :]), ALU.is_equal))
                        link(dve.tensor_copy(mk[:, k, :, :], m[:, :, :].rearrange("p t e -> p e t")))
                        link(dve.tensor_copy(mkf[:, k, :, :], m[:, :, :].rearrange("p t e -> p e t")))
                        link(dve.tensor_tensor(R["t0"][:, :, :], m[:, :, :], ind, ALU.mult))
                        link(dve.tensor_reduce(idx[:, k, :], R["t0"][:, :, :], AX.X, ALU.add))
                        if k == 0:
                            link(dve.tensor_scalar(R["t0"][:, :, :], m[:, :, :], -4.0, None, ALU.mult))
                            link(dve.tensor_tensor(R["q"][:, :, :], cur[:, :, :], R["t0"][:, :, :], ALU.add))
                            cur = R["q"]
                    dve.nop().then_inc(route_pe, 1)
                    link(dve.tensor_tensor(rc[:, 5, :], rc[:, 3, :], rc[:, 4, :], ALU.add))
                    link(dve.tensor_scalar(rc[:, 5, :], rc[:, 5, :], EPS_GATE, None, ALU.max))
                    link(dve.reciprocal(rc[:, 6, :], rc[:, 5, :]))
                    for k in range(2):
                        link(dve.tensor_tensor(gates[:, k, :], rc[:, 3 + k, :], rc[:, 6, :], ALU.mult))
                    dve.wait_ge(route_pe, 2)
                    flat = "p a b c -> p (a b) c"
                    first = bank(1)[:, 0:2 * E * NTT].rearrange("p (a b c) -> p a b c", a=2, b=E)
                    before = bank(0)[:, 0:2 * E * NTT].rearrange("p (a b c) -> p a b c", a=2, b=E)
                    link(dve.tensor_copy(tot[:, 0, :, :, :], first))
                    a = 0
                    step = 1
                    while step < NTT:
                        src = tot[:, a, :, :, :].rearrange(flat)
                        dst = tot[:, 1 - a, :, :, :].rearrange(flat)
                        dve.tensor_copy(dst[:, :, 0:step], src[:, :, 0:step])
                        link(dve.tensor_tensor(dst[:, :, step:], src[:, :, step:], src[:, :, 0:NTT - step], ALU.add))
                        a = 1 - a
                        step *= 2
                    link(dve.tensor_tensor(exc[:, :, :, :], tot[:, a, :, :, :], first, ALU.subtract))
                    link(dve.tensor_tensor(exc[:, 1, :, :], exc[:, 1, :, :],
                                           tot[:, a, 0, :, NTT - 1:NTT].to_broadcast([P, E, NTT]), ALU.add))
                    link(dve.tensor_tensor(exc[:, :, :, :], exc[:, :, :, :], before, ALU.add))
                    link(dve.tensor_tensor(exc[:, :, :, :], exc[:, :, :, :], mkf[:, :, :, :], ALU.mult))
                    for k in range(2):
                        link(dve.tensor_reduce(loc[:, k, :], exc[:, k, :, :].rearrange("p e t -> p t e"), AX.X,
                                               ALU.add))
                    link(dve.tensor_scalar(keep[:, :, :], loc[:, :, :], float(CAP), None, ALU.is_lt))
                    link(dve.tensor_tensor(gates[:, :, :], gates[:, :, :], keep[:, :, :], ALU.mult))
                    link(dve.tensor_scalar(idx[:, :, :], idx[:, :, :], float(CAP), float(-ROWS), ALU.mult, ALU.add))
                    link(dve.tensor_tensor(idx[:, :, :], idx[:, :, :], loc[:, :, :], ALU.add))
                    link(dve.tensor_tensor(idx[:, :, :], idx[:, :, :], keep[:, :, :], ALU.mult))
                    link(dve.tensor_scalar(idx[:, :, :], idx[:, :, :], float(ROWS), None, ALU.add))
                    dve.tensor_copy(posu[:, :, :], idx[:, :, :]).then_inc(routed, 1)
                    dve.wait_ge(wa_in, 16 * 6)
                    with dve.Fori(0, E // 2) as i:
                        def evac_rows(s):
                            for t in range(CT):
                                n = s * CT + t
                                dve.wait_ge(es["xT_mm"], n + 1)
                                dve.tensor_copy(dxT[:, s, :, t * P:(t + 1) * P],
                                                bank(6 + n % 2)[:, 0:KD * P].rearrange("p (k n) -> p k n", k=KD)
                                                ).then_inc(es["xT_done"], 1)

                        def evac_out(s):
                            for t in range(CT):
                                n = s * CT + t
                                dve.wait_ge(es["f2_mm"], n + 1)
                                if t == 0 and s:
                                    dve.wait_ge(es["y_out"], 16)
                                dve.tensor_tensor(ysb[:, t, :], bank(4 + n % 2)[:, 0:D], b2s[:, s, :],
                                                  ALU.add).then_inc(es["y_done"], 1)

                        evac_rows(0)
                        dve.wait_ge(es["wb_in"], 64)
                        evac_rows(1)
                        evac_out(0)
                        evac_out(1)
                        dve.wait_ge(es["y_done"], 2 * CT)
                        turn_ends(dve, go[1], i, e_arrived)

            yk = w1s[:, :, :, :].rearrange("p a b c -> p (a b c)")
            y_at = [yk.rearrange("p (t d) -> p t d", d=D), w2s[:, :, :, :].rearrange("p a b d -> p (a b) d")]
            xa = dx[:, 0, :, :]
            xb = dx[:, 1, :, :]
            n1 = hTe[:, :, :].rearrange("p m n -> p (m n)")[:, 0:NT * D].rearrange("p (t d) -> p t d", d=D)
            n2 = hTe[:, :, :].rearrange("p m n -> p (m n)")[:, NT * D:2 * NT * D].rearrange("p (t d) -> p t d", d=D)
            outv = out.rearrange("b (t p) d -> b p t d", p=P)
            with nc.Block() as block:
                @block.sync
                def _(sp):
                    with sp.Fori(0, B) as b:
                        sp.wait_ge(cs["fin_done"], NT)
                        sp.dma_start(outv[bass.ds(b, 1), :, :, :].rearrange("o p t d -> p (o t) d"),
                                     n2).then_inc(cs["out_done"], 16)
                        sp.wait_ge(cs["out_done"], 16)
                        turn_ends(sp, go[2], b, c_arrived, clear=combine_range)

                @block.gpsimd
                def _(pool):
                    for t in range(NTT):
                        for k in range(2):
                            pool.indirect_dma_start(
                                out=y_at[k][:, t, :], out_offset=None, in_=ydram,
                                in_offset=bass.IndirectOffsetOnAxis(ap=posu[:, k, t:t + 1], axis=0)
                            ).then_inc(gathered, 16)
                    with pool.Fori(0, B) as b:
                        for t in range(2 * NT):
                            pool.wait_ge(cs["cvar_done"], t + 1)
                            pool.tensor_tensor(rstd[:, t, 0:1], mv[:, t, 1:2], neg_half[:, 0:1],
                                               ALU.pow).then_inc(cs["crstd_done"], 1)
                        pool.wait_ge(cs["crstd_done"], 2 * NT)
                        turn_ends(pool, go[2], b, c_arrived)

                @block.scalar
                def _(act):
                    with act.Fori(0, B) as b:
                        turn_ends(act, go[2], b, c_arrived)

                @block.tensor
                def _(pe):
                    with pe.Fori(0, B) as b:
                        turn_ends(pe, go[2], b, c_arrived)

                @block.vector
                def _(dve):
                    dve.wait_ge(gathered, 16 * 2 * NTT)
                    done = [0]

                    def link(ins):
                        done[0] += 1
                        ins.then_inc(cs["c_chain"], 1)
                        dve.wait_ge(cs["c_chain"], done[0])

                    def moments(n, x):
                        link(dve.bn_stats(stat[:, n % 2, :], x))
                        link(dve.bn_aggr(mv[:, n, :], stat[:, n % 2, :]))
                        dve.tensor_scalar(mv[:, n, 1:2], mv[:, n, 1:2], EPS_LN, None,
                                          ALU.add).then_inc(cs["cvar_done"], 1)

                    with dve.Fori(0, B) as b:
                        def tile(v, t):
                            return v[:, bass.ds(b * NT + t, 1), :].rearrange("p o d -> p (o d)")

                        for t in range(NT):
                            g = [gates[:, k, bass.ds(b * NT + t, 1)] for k in range(2)]
                            link(dve.tensor_scalar(xa[:, t, :], tile(y_at[0], t), g[0], None, ALU.mult))
                            link(dve.scalar_tensor_tensor(xa[:, t, :], tile(y_at[1], t), g[1], xa[:, t, :], ALU.mult,
                                                          ALU.add))
                            link(dve.tensor_tensor(xa[:, t, :], xa[:, t, :], tile(h3, t), ALU.add))
                            moments(t, xa[:, t, :])
                        for t in range(NT):
                            dve.wait_ge(cs["crstd_done"], t + 1)
                            link(dve.tensor_scalar(n1[:, t, :], xa[:, t, :], mv[:, t, 0:1], rstd[:, t, 0:1],
                                                   ALU.subtract, ALU.mult))
                            link(dve.tensor_tensor(n1[:, t, :], n1[:, t, :], lnr[:, 0:D], ALU.mult))
                            link(dve.tensor_tensor(n1[:, t, :], n1[:, t, :], lnr[:, D:2 * D], ALU.add))
                            link(dve.tensor_tensor(xb[:, t, :], n1[:, t, :], tile(h3, t), ALU.add))
                            moments(NT + t, xb[:, t, :])
                        for t in range(NT):
                            dve.wait_ge(cs["crstd_done"], NT + t + 1)
                            dve.tensor_scalar(n2[:, t, :], xb[:, t, :], mv[:, NT + t, 0:1], rstd[:, NT + t, 0:1],
                                              ALU.subtract, ALU.mult).then_inc(cs["fin_done"], 1)
                        dve.wait_ge(cs["fin_done"], NT)
                        turn_ends(dve, go[2], b, c_arrived)
                        done[0] = 0


def kernel(**inputs):
    import concourse.bacc as _bacc
    from concourse.bass_utils import run_bass_kernel_spmd as _run

    a = {k: np.asarray(v) for k, v in inputs.items()}

    def rows(w):
        return w.reshape(-1, P, w.shape[1]).transpose(1, 0, 2)

    def pad_heads(w):
        o = np.zeros(w.shape[:-1] + (H, SLOT), w.dtype)
        o[..., :DH] = w.reshape(w.shape[:-1] + (H, DH))
        return o.reshape(w.shape[:-1] + (H * SLOT,))

    def bias_cols(b, fill):
        o = pad_heads(b).reshape(H, SLOT)
        if fill:
            o[:, AUG] = 1.0
        return o.reshape(NG, P).T

    def wide(*vs):
        return np.broadcast_to(np.concatenate(vs)[None], (P, sum(v.size for v in vs)))

    wattn, wo, battn, brow = [], [], [], []
    for l in range(2):
        w = {n: (a[f"L{l}_attn_W{n}"] if l == 0 else a[f"L{l}_attn_W{n}"].T) for n in "qkvo"}
        bias = {n: a[f"L{l}_attn_b{n}"] for n in "qkvo"}
        wattn.append(rows(np.concatenate([pad_heads(w["q"]), pad_heads(w["k"]), w["v"]], axis=1)))
        wo.append(rows(w["o"]))
        battn.append(np.concatenate([bias_cols(bias["q"], False), bias_cols(bias["k"], True)], axis=1))
        brow.append(wide(bias["v"], bias["o"]))

    p = np.arange(P)[:, None]
    c = np.arange(S)[None, :]
    consts = np.zeros((P, C_END), np.float32)
    consts[:, C_ID:C_ID + P] = np.eye(P)
    consts[:, C_CM:C_CM + S] = np.where(c - (S - P) > p, MASKED, 0.0)
    w = np.arange(2 * P)[None, :] - HALF_WINDOW
    consts[:, C_WM:C_WM + 2 * P] = np.where(np.abs(w - p) > HALF_WINDOW, MASKED, 0.0)
    consts[:, C_TRI:C_TRI + P] = p < np.arange(P)[None, :]
    consts[:, C_ONE:C_ONE + P] = 1.0
    consts[:, C_REV:C_REV + P] = E - np.arange(P)[None, :] % E
    consts[:, C_IDX:C_IDX + P] = np.arange(P)[None, :] % E

    ins = {
        "xT": a["x"].transpose(3, 2, 0, 1).reshape(4, D, N),
        "w01": rows(np.concatenate([a["L0_tok_W0"].T, a["L0_tok_W1"].T], axis=1)),
        "wtok": rows(a["L0_tok_Wo"].T),
        "wattn": np.stack(wattn), "wo": np.stack(wo), "battn": np.stack(battn), "brow": np.stack(brow),
        "wq0": np.stack([rows(a["L0_ffn_w_gate"].T).reshape(P, -1), rows(a["L0_ffn_w_up"].T).reshape(P, -1)]),
        "wdn": rows(a["L0_ffn_w_down"].T).reshape(P, -1),
        "wgate": rows(a["L1_ffn_wg"]),
        "consts": consts,
        "w1": a["L1_ffn_fc1_w"].transpose(0, 2, 1).reshape(E, KD, P, HE).transpose(0, 2, 1, 3),
        "w2": a["L1_ffn_fc2_w"].reshape(E, MH, P, D).transpose(0, 2, 1, 3),
        "b1": a["L1_ffn_fc1_b"].reshape(E, MH, P).transpose(2, 0, 1),
        "b2": np.broadcast_to(a["L1_ffn_fc2_b"][:, None, :], (E, P, D)),
        "lnrow": wide(a["L1_ffn_ln_gamma"], a["L1_ffn_ln_beta"]),
    }
    ins = {n: np.ascontiguousarray(v) for n, v in ins.items()}
    nc = _bacc.Bacc("TRN2", target_bir_lowering=False, num_devices=1)
    aps = [nc.dram_tensor(n, v.shape, mybir.dt.from_np(v.dtype), kind="ExternalInput").ap() for n, v in ins.items()]
    out = nc.dram_tensor("out", (B, S, D), F32, kind="ExternalOutput").ap()
    build(nc, *aps, out)
    return _run(nc, [ins], core_ids=[0]).results[0]["out"]
```

```python
from contextlib import ExitStack

import concourse.bass as bass
import numpy as np
from concourse import mybir

F32 = mybir.dt.float32
BF16 = mybir.dt.bfloat16
U32 = mybir.dt.uint32
ALU = mybir.AluOpType
ACT = mybir.ActivationFunctionType
AX = mybir.AxisListType

P = 128
B, S, D = 4, 512, 256
N = B * S
KD = D // P
NT = S // P
NTT = N // P
DE = 512
ME = DE // P
H, DH = 16, 16
SLOT = 32
HG = P // SLOT
NG = H // HG
HB = P // DH
NB = H // HB
Q_PARTS = (0, 0, 1, 0, 2, 1)
K_PARTS = (0, 1, 0, 2, 0, 1)
KS = len(Q_PARTS) * DH
KM = KS + 3
HALF_WINDOW = 64
I0 = 1024
MI = I0 // P
E, HE = 8, 1024
MH = HE // P
CAP = 2 * int(1.25 * ((N + E - 1) // E))
CT = CAP // P
ROWS = E * CAP
HC = CAP // 2
EPS_LN = 1e-5
EPS_Q = 1e-5
EPS_GATE = 1.1920929e-07
MAGIC = 1.5 * 2.0 ** 23
MASKED = -1.0e30

C_ID, C_TRI, C_ONE, C_REV, C_IDX, C_END = 0, 128, 256, 384, 512, 640
M_CAUSAL, M_WINDOW, M_END = 0, S, S + 2 * P
WINDOW, CAUSAL = 0, 1
LAG, TURN = 5, 2


def q_range(kind, kt):
    if kind == CAUSAL:
        return kt * P, S
    return max(0, kt * P - HALF_WINDOW), min(S, (kt + 1) * P + HALF_WINDOW)


def k_range(kind, t):
    if kind == CAUSAL:
        return 0, (t + 1) * P
    return max(0, t * P - HALF_WINDOW), min(S, (t + 1) * P + HALF_WINDOW)


def build(nc, xT, w01, wtok, wattn, wo, battn, brow, wq0, wdn, wgate, consts, masks, w1, w2, b1, b2, lnrow, out):
    disp = nc.dram_tensor("dispatched_rows", (ROWS, D), F32, kind="Internal").ap()
    ydram = nc.dram_tensor("expert_rows", (ROWS + P, D), F32, kind="Internal").ap()
    ctx = ExitStack()
    with ctx:
        def sb(name, shape, dt=F32):
            return ctx.enter_context(nc.sbuf_tensor(name, shape, dt))

        def sem(name):
            return ctx.enter_context(nc.semaphore(name))

        cst = sb("cst", [P, C_END])
        identb = sb("identb", [P, P], BF16)
        trib = sb("trib", [P, 2 * P], BF16)
        maskb = sb("maskb", [P, M_END], BF16)
        tokw = sb("tokw", [P, KD, 2 * DE])
        tokwo = sb("tokwo", [P, ME, D])
        aw = [sb(f"aw{l}", [P, KD, 3 * D]) for l in range(2)]
        awo = [sb(f"awo{l}", [P, KD, D]) for l in range(2)]
        ab = [sb(f"ab{l}", [P, 2 * NB]) for l in range(2)]
        ar = [sb(f"ar{l}", [P, 2 * D]) for l in range(2)]
        qgu = sb("qgu", [P, KD, 2 * I0], BF16)
        qdn = sb("qdn", [P, MI, D], BF16)
        gatew = sb("gatew", [P, KD, E])
        h3 = sb("h3", [P, NTT, D])
        logits = sb("logits", [P, NTT, E])
        x_sb = sb("x_sb", [P, KD, S])
        h = sb("h", [P, NT, D])
        res = sb("res", [P, NT, D])
        hT = sb("hT", [P, KD, S])
        att = sb("att", [P, NT, D])
        attT = sb("attT", [P, KD, S])
        lnx = att
        stat = sb("stat", [P, 4, 6])
        mv = sb("mv", [P, NTT, 2])
        rstd = sb("rstd", [P, NTT, 2])
        small = sb("small", [P, 32])
        wsc = sb("wsc", [P, 16])
        neg_half = sb("neg_half", [P, 4])

        ident = cst[:, C_ID:C_ID + P]
        ones = cst[:, C_ONE:C_ONE + P]

        ps = ctx.enter_context(nc.psum_tensor("ps", [P, 8, 512], F32))

        def bank(i):
            return ps[:, i, :]

        for_x, for_tok, for_attn, for_ffn, for_cst = (sem(n) for n in (
            "for_x", "for_tok", "for_attn", "for_ffn", "for_cst"))
        prep = sem("prep")
        prep_act = sem("prep_act")
        prep_pe = sem("prep_pe")
        prep_pool = sem("prep_pool")
        zeroed = sem("zeroed")
        routed = sem("routed")
        route_pe = sem("route_pe")
        route_act = sem("route_act")
        dve_route = sem("dve_route")
        scattered = sem("scattered")
        gathered = sem("gathered")
        stored = sem("stored")
        wa_in = sem("wa_in")
        go = [sem(f"go{i}") for i in range(3)]

        arrived = sem("arrived")
        bs = {n: sem(n) for n in (
            "gu_mm", "relu_done", "hid_done", "h0_mm", "h0_done",
            "hT_mm0", "hT_done0", "hT_mm1", "hT_done1", "hT_mm2", "hT_done2",
            "fq_done", "fq_mm", "fqT_done", "fgu_mm", "fsq_done", "fh_done", "fq2_done", "fq2_mm", "fq2T_done",
            "fdn_mm", "lg_mm", "lg_done", "x_in", "keep_done", "dve_chain", "act_chain", "pool_chain")}
        for l in range(2):
            for n in ("qk_mm", "ev_done", "p1_done", "rest_done", "p2_done", "part_done", "stack_in0", "stack_in1",
                      "nmax_in0", "nmax_in1", "nparts_done", "nrow_done", "v_mm", "v_done", "s_mm", "max_done", "nm_mm",
                      "st_mm", "exp_done", "sel_done", "pv_mm", "ot_done", "ob_mm", "o_done", "oT_mm", "oT_done",
                      "pr_mm", "res_done"):
                bs[f"{n}{l}"] = sem(f"{n}{l}")
        for l in range(3):
            for n in ("lns_done", "var_done", "rstd_done", "ln_done"):
                bs[f"{n}{l}"] = sem(f"{n}{l}")
        batch_range = range(arrived.num, max(s.num for s in bs.values()) + 1)
        assert len(batch_range) == len(bs) + 1

        e_arrived = sem("e_arrived")
        es = {n: sem(n) for n in ("wb_in", "xT_mm", "xT_done", "f1_mm", "silu_done", "f2_mm", "y_done", "y_out",
                                  "wa_next")}
        expert_range = range(e_arrived.num, max(s.num for s in es.values()) + 1)
        assert len(expert_range) == len(es) + 1

        c_arrived = sem("c_arrived")
        cs = {n: sem(n) for n in ("mix_done", "cvar_done", "crstd_done", "cn_done", "out_done", "c_chain",
                                  "fin_done")}
        combine_range = range(c_arrived.num, max(s.num for s in cs.values()) + 1)
        assert len(combine_range) == len(cs) + 1

        def turn_ends(eng, gate, turn, counter, clear=None):
            if clear is not None:
                eng.wait_ge(counter, 4)
                eng.sem_clear(clear)
                eng.sem_inc(gate, 1)
            else:
                eng.sem_inc(counter, 1)
                eng.wait_ge(gate, turn + 1)

        with ExitStack() as c2:
            def sb2(name, shape, dt=F32):
                return c2.enter_context(nc.sbuf_tensor(name, shape, dt))

            relu_g = att[:, :, :].rearrange("p (a t) d -> p a (t d)", a=2)
            hid = sb2("hid", [P, ME, S])
            qs = sb2("qs", [P, H, S], BF16)
            ks = sb2("ks", [P, H, S], BF16)
            proj = sb2("proj", [P, 2, S])
            parts = sb2("parts", [P, 2 * NB, 3, S], BF16)
            vaug = sb2("vaug", [P, NT, H * SLOT])
            nmax = sb2("nmax", [P, 2, HG, NT])
            nrest = sb2("nrest", [P, HG, NT])
            nparts = sb2("nparts", [P, 2, NT, 3 * HG], BF16)
            nrows = sb2("nrows", [3 * HG, 2, S], BF16)
            junk = sb2("junk", [P, 2, S], BF16)
            probs = sb2("probs", [P, 3, HG, S])
            oT = sb2("oT", [P, NG, S])
            rsum = sb2("rsum", [P, NT, H])
            fq = sb2("fq", [P, D])
            fqb = sb2("fqb", [P, 2, D], BF16)
            fqT = sb2("fqT", [P, 2, KD, P], BF16)
            fr = hid[:, 0:2, :].rearrange("p a n -> p (a n)")
            fsq = hid[:, 2:4, :].rearrange("p a n -> p (a n)")
            fh = sb2("fh", [P, I0])
            fq2 = sb2("fq2", [P, I0], BF16)
            fq2T = sb2("fq2T", [P, MI, P], BF16)
            zero_rows = h3[:, NTT - 2:NTT, :]
            wgu_f = [v[:, :, :].rearrange("p g s -> p (g s)").bitcast(F32)[:, 0:KD * I0] for v in (qs, ks)]
            wdn_f = oT[:, :, :].rearrange("p g s -> p (g s)")

            with nc.Block() as block:
                @block.sync
                def _(sp):
                    for n in range(2):
                        sp.dma_start(wgu_f[n], wq0[n]).then_inc(for_ffn, 16)
                    sp.dma_start(wdn_f, wdn).then_inc(for_ffn, 16)
                    for k in range(KD):
                        sp.dma_start(tokw[:, k, :], w01[:, k, :]).then_inc(for_tok, 16)
                        sp.dma_start(x_sb[:, k, :], xT[0, k * P:(k + 1) * P, 0:S]).then_inc(for_x, 16)
                    sp.dma_start(tokwo[:, :, :], wtok).then_inc(for_tok, 16)
                    sp.wait_ge(prep_pool, 1)
                    for c in range(ROWS // (2 * P)):
                        sp.dma_start(disp[c * 2 * P:(c + 1) * 2 * P, :].rearrange("(p r) d -> p r d", r=2),
                                     zero_rows).then_inc(zeroed, 16)
                    sp.dma_start(ydram[ROWS:ROWS + P, :], zero_rows[:, 0, :]).then_inc(zeroed, 16)

                    def stack(l):
                        for blk in range(NB):
                            for part, ready in enumerate(("p1_done", "p2_done", "part_done")):
                                for is_k in range(2):
                                    i = 2 * blk + is_k
                                    sp.wait_ge(bs[f"{ready}{l}"], i + 1)
                                    dst, order = (ks, K_PARTS) if is_k else (qs, Q_PARTS)
                                    for r in range(len(order)):
                                        if order[r] == part:
                                            sp.dma_start(dst[r * DH:(r + 1) * DH, blk * HB:(blk + 1) * HB, :],
                                                         parts[:, i, part, :]).then_inc(bs[f"stack_in{blk}{l}"], 16)
                        for g in range(NG):
                            sp.wait_ge(bs[f"nrow_done{l}"], g + 1)
                            sp.dma_start(qs[KS:KM, g * HG:(g + 1) * HG, :], nrows[:, g % 2, :]
                                         ).then_inc(bs[f"nmax_in{g % 2}{l}"], 16)

                    with sp.Fori(0, B) as b:
                        sp.wait_ge(bs["gu_mm"], ME)
                        sp.dma_start(x_sb[:, :, :], xT[0, :, bass.ds((b + 1) % B * S, S)].rearrange(
                            "(k p) n -> p k n", p=P)).then_inc(bs["x_in"], 16)
                        stack(0)
                        stack(1)
                        sp.wait_ge(bs["x_in"], 16)
                        turn_ends(sp, go[0], b, arrived, clear=batch_range)

                @block.gpsimd
                def _(pool):
                    pool.memset(zero_rows[:, :, :], 0.0).then_inc(prep_pool, 1)
                    pool.memset(neg_half[:, :], -0.5)
                    pool.memset(vaug[:, :, :], 0.0).then_inc(prep_pool, 1)
                    pool.wait_ge(prep_pool, 2)
                    pool.memset(vaug[:, :, :].rearrange("p t (h s) -> p (t h) s", s=SLOT)[:, :, DH:DH + 1],
                                1.0).then_inc(prep_pool, 1)

                    def second_parts(l):
                        for i in range(2 * NB):
                            pool.wait_ge(bs[f"rest_done{l}"], i + 1)
                            pool.tensor_copy(parts[:, i, 1, :], proj[:, i % 2, :]).then_inc(bs[f"p2_done{l}"], 1)

                    def residual(l, ready, count):
                        for t in range(NT):
                            if ready is not None:
                                pool.wait_ge(bs[ready], count + t)
                            pool.tensor_tensor(res[:, t, :], h[:, t, :], ar[l][:, D:2 * D],
                                               ALU.add).then_inc(bs[f"res_done{l}"], 1)

                    def select(kind, l):
                        for u in range(NG * NT):
                            kt = u % NT
                            lo, hi = q_range(kind, kt)
                            pool.wait_ge(bs[f"exp_done{l}"], 2 * u + 2)
                            cuts = []
                            if kind == CAUSAL:
                                cuts.append((0, P, 0, 1, -1))
                            else:
                                cut = kt * P + HALF_WINDOW - lo
                                cuts.append((0, cut, lo - kt * P + HALF_WINDOW, 1, -1))
                                cuts.append((cut, hi - lo, 0, -1, 1))
                            for i, (a, z, base, step, mult) in enumerate(cuts):
                                part = probs[:, u % 3, :, a:z]
                                ins = pool.affine_select(out=part, in_=part, compare_op=ALU.is_ge, fill=0.0,
                                                         base=base, pattern=[[0, HG], [step, z - a]],
                                                         channel_multiplier=mult)
                            ins.then_inc(bs[f"sel_done{l}"], 1)

                    def rstds(n, rows):
                        for t in range(rows):
                            pool.wait_ge(bs[f"var_done{n}"], t + 1)
                            pool.tensor_tensor(rstd[:, t, 0:1], mv[:, t, 1:2], neg_half[:, 0:1],
                                               ALU.pow).then_inc(bs[f"rstd_done{n}"], 1)

                    with pool.Fori(0, B) as b:
                        pool.wait_ge(for_attn, 16 * 8)
                        second_parts(0)
                        residual(0, "h0_done", 1)
                        select(WINDOW, 0)
                        rstds(0, NT)
                        rstds(1, NT)
                        second_parts(1)
                        residual(1, "ln_done1", 1)
                        select(CAUSAL, 1)
                        rstds(2, NT)
                        pool.wait_ge(zeroed, 16 * (ROWS // (2 * P) + 1))
                        for t in range(NT):
                            pool.wait_ge(bs["ln_done2"], t + 1)
                            pool.tensor_copy(h3[:, bass.ds(b * NT + t, 1), :], h[:, t:t + 1, :]
                                             ).then_inc(bs["keep_done"], 1)
                        pool.wait_ge(bs["keep_done"], NT)
                        turn_ends(pool, go[0], b, arrived)

                @block.scalar
                def _(act):
                    act.dma_start(cst[:, :], consts).then_inc(for_cst, 16)
                    act.dma_start(fh[:, 0:M_END], masks).then_inc(for_cst, 16)
                    for l in range(2):
                        act.dma_start(aw[l][:, :, :], wattn[l]).then_inc(for_attn, 16)
                        act.dma_start(awo[l][:, :, :], wo[l]).then_inc(for_attn, 16)
                        act.dma_start(ab[l][:, :], battn[l]).then_inc(for_attn, 16)
                        act.dma_start(ar[l][:, :], brow[l]).then_inc(for_attn, 16)
                    act.dma_start(gatew[:, :, :], wgate).then_inc(for_cst, 16)

                    def turned(n, l):
                        for t in range(NT):
                            act.wait_ge(bs[f"hT_mm{n}"], t + 1)
                            act.activation(hT[:, :, t * P:(t + 1) * P],
                                           bank(6 + t % 2)[:, 0:KD * P].rearrange("p (k n) -> p k n", k=KD),
                                           ACT.Copy).then_inc(bs[f"hT_done{n}"], 1)

                    def attention(kind, l):
                        for i in range(2 * NB):
                            act.wait_ge(bs[f"qk_mm{l}"], i + 1)
                            if i >= 2:
                                act.wait_ge(bs[f"part_done{l}"], i - 1)
                            kw = dict(bias=ab[l][:, i:i + 1], scale=1.0 if i % 2 else DH ** -0.5)
                            act.activation(proj[:, i % 2, :], bank(i % 4), ACT.Identity,
                                           **kw).then_inc(bs[f"ev_done{l}"], 1)
                            act.activation(parts[:, i, 0, :], bank(i % 4), ACT.Identity,
                                           **kw).then_inc(bs[f"p1_done{l}"], 1)
                        def maxima_rows(g):
                            act.wait_ge(bs[f"nm_mm{l}"], g + 1)
                            if g >= 2:
                                act.wait_ge(bs[f"nmax_in{g % 2}{l}"], 16 * (g // 2))
                            act.activation(nrows[:, g % 2, :], bank(7).bitcast(BF16)[0:3 * HG, 0:S],
                                           ACT.Copy).then_inc(bs[f"nrow_done{l}"], 1)

                        for u in range(NG * NT):
                            g, kt = divmod(u, NT)
                            lo, hi = q_range(kind, kt)
                            if u == 0:
                                maxima_rows(0)
                            if u >= 3:
                                act.wait_ge(bs[f"pv_mm{l}"], u - 2)
                            for half in range(2):
                                v = 2 * u + half
                                pair = 2 * (1 - half)
                                if (v + LAG - TURN) % (2 * NT) == 0 and v < 2 * NT * (NG - 1):
                                    maxima_rows((v + LAG - TURN) // (2 * NT))
                                act.wait_ge(bs[f"st_mm{l}"], v + 1)
                                act.activation(probs[:, u % 3, pair:pair + 2, 0:hi - lo],
                                               ps[:, 2 * (v % 2):2 * (v % 2) + 2, 0:hi - lo],
                                               ACT.Exp).then_inc(bs[f"exp_done{l}"], 1)
                            if kt == 1 and g:
                                act.wait_ge(bs[f"pv_mm{l}"], NT * g)
                                act.activation(oT[:, g - 1, :], bank(6), ACT.Copy).then_inc(bs[f"ot_done{l}"], 1)
                        act.wait_ge(bs[f"pv_mm{l}"], NT * NG)
                        act.activation(oT[:, NG - 1, :], bank(6), ACT.Copy).then_inc(bs[f"ot_done{l}"], 1)
                        for t in range(NT):
                            act.wait_ge(bs[f"oT_mm{l}"], t + 1)
                            act.activation(attT[:, :, t * P:(t + 1) * P],
                                           bank(6 + t % 2)[:, 0:KD * P].rearrange("p (k n) -> p k n", k=KD),
                                           ACT.Copy).then_inc(bs[f"oT_done{l}"], 1)

                    with act.Fori(0, B) as b:
                        for m in range(ME):
                            act.wait_ge(bs["gu_mm"], m + 1)
                            if m >= 2:
                                act.wait_ge(bs["hid_done"], m - 1)
                            act.activation(relu_g[:, m % 2, :], bank(2 * (m % 2)),
                                           ACT.Relu).then_inc(bs["relu_done"], 1)
                        turned(0, 0)
                        act.wait_ge(for_attn, 16 * 8)
                        attention(WINDOW, 0)
                        def gate_squares(t):
                            act.wait_ge(bs["fq_mm"], t + 1)
                            if t >= 2:
                                act.wait_ge(bs["fgu_mm"], t - 1)
                            act.activation(fqT[:, t % 2, :, :],
                                           bank(6 + t % 2).bitcast(BF16)[:, 0:KD * P].rearrange(
                                               "p (k n) -> p k n", k=KD), ACT.Copy).then_inc(bs["fqT_done"], 1)
                            act.wait_ge(bs["fgu_mm"], t + 1)
                            act.activation(hid[:, 0:2, :], ps[:, 0:2, :],
                                           ACT.Relu).then_inc(bs["act_chain"], 1)
                            act.wait_ge(bs["act_chain"], t + 1)
                            if t:
                                act.wait_ge(bs["fh_done"], t)
                            act.activation(fsq, fr, ACT.Square).then_inc(bs["fsq_done"], 1)

                        gate_squares(0)
                        for t in range(NT):
                            if t + 1 < NT:
                                gate_squares(t + 1)
                            act.wait_ge(bs["fq2_mm"], t + 1)
                            if t:
                                act.wait_ge(bs["fdn_mm"], t)
                            act.activation(fq2T[:, :, :],
                                           bank(4).bitcast(BF16).rearrange("p (k n) -> p k n", k=MI),
                                           ACT.Copy).then_inc(bs["fq2T_done"], 1)
                        turned(1, 0)
                        attention(CAUSAL, 1)
                        turned(2, 0)
                        act.wait_ge(bs["hT_done2"], NT)
                        turn_ends(act, go[0], b, arrived)

                @block.tensor
                def _(pe):
                    mm = pe.matmul

                    def turn(n, ready):
                        def one(t):
                            pe.wait_ge(bs[ready], t + 1)
                            if t >= 2:
                                pe.wait_ge(bs[f"hT_done{n}"], t - 1)
                            for k in range(KD):
                                ins = pe.transpose(bank(6 + t % 2)[:, k * P:(k + 1) * P],
                                                   h[:, t, k * P:(k + 1) * P], ident)
                            ins.then_inc(bs[f"hT_mm{n}"], 1)
                        return one

                    def attention(kind, l, hT_ready):
                        w = aw[l]
                        pe.wait_ge(bs[hT_ready], NT)

                        def queries_keys(blk):
                            for is_k in range(2):
                                i = 2 * blk + is_k
                                c = (is_k * NB + blk) * P
                                for k in range(KD):
                                    ins = mm(bank(i % 4), w[:, k, c:c + P], hT[:, k, :], start=(k == 0),
                                             stop=(k == KD - 1))
                                ins.then_inc(bs[f"qk_mm{l}"], 1)

                        queries_keys(0)
                        for t in range(NT):
                            if t >= 2:
                                pe.wait_ge(bs[f"v_done{l}"], t - 1)
                            for k in range(KD):
                                ins = mm(bank(4 + t % 2)[:, 0:D], hT[:, k, t * P:(t + 1) * P],
                                         w[:, k, 2 * D:], start=(k == 0), stop=(k == KD - 1))
                            ins.then_inc(bs[f"v_mm{l}"], 1)
                        queries_keys(1)
                        pe.wait_ge(bs[f"v_done{l}"], NT)

                        def scores(g, t, pair):
                            if t == 0 and pair == 0:
                                blk = g * HG // HB
                                pe.wait_ge(bs[f"stack_in{blk}{l}"], 16 * 2 * len(Q_PARTS))
                            lo, hi = k_range(kind, t)
                            for j in (pair, pair + 1):
                                i = g * NT * HG + t * HG + j
                                if i >= 2:
                                    pe.wait_ge(bs[f"max_done{l}"], i - 1)
                                hd = g * HG + j
                                mm(bank(4 + j % 2)[:, 0:hi - lo], qs[0:KS, hd, t * P:(t + 1) * P],
                                   ks[0:KS, hd, lo:hi], start=True, stop=True).then_inc(bs[f"s_mm{l}"], 1)

                        def maxima(g):
                            pe.wait_ge(bs[f"nparts_done{l}"], g + 1)
                            if g:
                                pe.wait_ge(bs[f"nrow_done{l}"], g)
                            for t in range(NT):
                                ins = pe.transpose(bank(7).bitcast(BF16)[0:3 * HG, t * P:(t + 1) * P],
                                                   nparts[:, g % 2, t, :], identb[:, :])
                            ins.then_inc(bs[f"nm_mm{l}"], 1)

                        def scores_T(g, kt, half):
                            u = g * NT + kt
                            v = 2 * u + half
                            pair = 2 * (1 - half)
                            lo, hi = q_range(kind, kt)
                            if kt == 0 and half == 0:
                                pe.wait_ge(bs[f"nmax_in{g % 2}{l}"], 16 * (g // 2 + 1))
                            if v >= 2:
                                pe.wait_ge(bs[f"exp_done{l}"], v - 1)
                            for i in range(2):
                                j = pair + i
                                hd = g * HG + j
                                ins = mm(bank(2 * (v % 2) + i)[:, 0:hi - lo], ks[0:KM, hd, kt * P:(kt + 1) * P],
                                         qs[0:KM, hd, lo:hi], start=True, stop=True)
                            ins.then_inc(bs[f"st_mm{l}"], 1)

                        def values(g, kt):
                            u = g * NT + kt
                            lo, hi = q_range(kind, kt)
                            pe.wait_ge(bs[f"sel_done{l}"], u + 1)
                            if kt == 0 and g:
                                pe.wait_ge(bs[f"ot_done{l}"], g)
                            for j in range(HG):
                                hd = g * HG + j
                                ins = mm(bank(6)[SLOT * j:SLOT * j + SLOT, lo:hi],
                                         vaug[:, kt, hd * SLOT:(hd + 1) * SLOT], probs[:, u % 3, j, 0:hi - lo],
                                         start=(kt == 0), stop=(kt == NT - 1), skip_group_check=True,
                                         tile_position=(0, SLOT * j))
                            ins.then_inc(bs[f"pv_mm{l}"], 1)

                        late = []
                        for step in range(2 * NT * NG + 2 * NT + LAG):
                            g, r = divmod(step, 2 * NT)
                            if g < NG:
                                scores(g, r // 2, 2 * (r % 2))
                            if r == TURN and 1 <= g <= NG:
                                maxima(g - 1)
                            v = step - 2 * NT - LAG
                            if v >= 0:
                                u, half = divmod(v, 2)
                                scores_T(u // NT, u % NT, half)
                                if half == 1:
                                    late.append((u // NT, u % NT))
                                elif len(late) == 2:
                                    values(*late.pop(0))
                        for u in late:
                            values(*u)

                        def heads_back(t):
                            if t == 0:
                                pe.wait_ge(bs[f"ot_done{l}"], NG)
                            if t >= 2:
                                pe.wait_ge(bs[f"o_done{l}"], t - 1)
                            for g in range(NG):
                                ins = pe.transpose(bank(4 + t % 2)[:, g * P:(g + 1) * P],
                                                   oT[:, g, t * P:(t + 1) * P], ident)
                            ins.then_inc(bs[f"ob_mm{l}"], 1)

                        def heads_turn(t):
                            pe.wait_ge(bs[f"o_done{l}"], t + 1)
                            if t >= 2:
                                pe.wait_ge(bs[f"oT_done{l}"], t - 1)
                            for k in range(KD):
                                ins = pe.transpose(bank(6 + t % 2)[:, k * P:(k + 1) * P],
                                                   att[:, t, k * P:(k + 1) * P], ident)
                            ins.then_inc(bs[f"oT_mm{l}"], 1)

                        def project(t):
                            pe.wait_ge(bs[f"oT_done{l}"], t + 1)
                            if t >= 2:
                                pe.wait_ge(bs[f"lns_done{2 * l}"], t - 1)
                            for k in range(KD):
                                ins = mm(bank(t % 2)[:, 0:D], attT[:, k, t * P:(t + 1) * P], awo[l][:, k, :],
                                         start=(k == 0), stop=(k == KD - 1))
                            ins.then_inc(bs[f"pr_mm{l}"], 1)

                        for s in range(NT + 2):
                            if s < NT:
                                heads_back(s)
                            if 1 <= s < NT + 1:
                                heads_turn(s - 1)
                            if s >= 2:
                                project(s - 2)

                    pe.wait_ge(prep, 1)
                    mm(bank(7)[:, 0:4], ones, wsc[:, 0:4], start=True, stop=True).then_inc(prep_pe, 1)
                    pe.wait_ge(for_x, 16 * 2)
                    pe.wait_ge(for_tok, 16 * 3)
                    pe.wait_ge(for_cst, 16 * 3)
                    pe.wait_ge(prep_pool, 3)
                    pe.wait_ge(prep, 2)
                    with pe.Fori(0, B) as b:
                        for m in range(ME):
                            if m >= 2:
                                pe.wait_ge(bs["hid_done"], m - 1)
                            for n in range(2):
                                c = n * DE + m * P
                                for k in range(KD):
                                    ins = mm(bank(2 * (m % 2) + n), tokw[:, k, c:c + P], x_sb[:, k, :],
                                             start=(k == 0), stop=(k == KD - 1))
                            ins.then_inc(bs["gu_mm"], 1)
                        turn0 = turn(0, "h0_done")
                        pe.wait_ge(bs["hid_done"], ME)
                        for t in range(NT + 1):
                            if t < NT:
                                if t >= 2:
                                    pe.wait_ge(bs["h0_done"], t - 1)
                                for m in range(ME):
                                    ins = mm(bank(4 + t % 2)[:, 0:D], hid[:, m, t * P:(t + 1) * P], tokwo[:, m, :],
                                             start=(m == 0), stop=(m == ME - 1))
                                ins.then_inc(bs["h0_mm"], 1)
                            if t:
                                turn0(t - 1)
                        pe.wait_ge(for_attn, 16 * 8)
                        attention(WINDOW, 0, "hT_done0")

                        def f_turn(t):
                            pe.wait_ge(bs["fq_done"], t + 1)
                            if t >= 2:
                                pe.wait_ge(bs["fqT_done"], t - 1)
                            for k in range(KD):
                                ins = pe.transpose(bank(6 + t % 2).bitcast(BF16)[:, k * P:(k + 1) * P],
                                                   fqb[:, t % 2, k * P:(k + 1) * P], identb[:, :])
                            ins.then_inc(bs["fq_mm"], 1)

                        def f_up(t):
                            pe.wait_ge(bs["fqT_done"], t + 1)
                            if t:
                                pe.wait_ge(bs["fh_done"], t)
                            else:
                                pe.wait_ge(bs["lns_done0"], NT)
                            for n in range(4):
                                for k in range(KD):
                                    ins = mm(bank(n), fqT[:, t % 2, k, :], qgu[:, k, n * 512:(n + 1) * 512],
                                             start=(k == 0), stop=(k == KD - 1))
                            ins.then_inc(bs["fgu_mm"], 1)

                        def f_turn2(t):
                            pe.wait_ge(bs["fq2_done"], t + 1)
                            if t:
                                pe.wait_ge(bs["fq2T_done"], t)
                            for k in range(MI):
                                ins = pe.transpose(bank(4).bitcast(BF16)[:, k * P:(k + 1) * P],
                                                   fq2[:, k * P:(k + 1) * P], identb[:, :])
                            ins.then_inc(bs["fq2_mm"], 1)

                        def f_down(t):
                            pe.wait_ge(bs["fq2T_done"], t + 1)
                            if t:
                                pe.wait_ge(bs["lns_done1"], t)
                            for k in range(MI):
                                ins = mm(bank(5)[:, 0:D], fq2T[:, k, :], qdn[:, k, :], start=(k == 0),
                                         stop=(k == MI - 1))
                            ins.then_inc(bs["fdn_mm"], 1)

                        turn1 = turn(1, "ln_done1")
                        f_turn(0)
                        f_up(0)
                        for t in range(NT):
                            if t + 1 < NT:
                                f_turn(t + 1)
                                f_up(t + 1)
                            f_turn2(t)
                            f_down(t)
                        for t in range(NT):
                            turn1(t)
                        attention(CAUSAL, 1, "hT_done1")
                        turn2 = turn(2, "ln_done2")
                        for t in range(NT):
                            turn2(t)
                        pe.wait_ge(bs["hT_done2"], NT)
                        for t in range(NT):
                            for k in range(KD):
                                ins = mm(bank(4)[:, t * E:(t + 1) * E], hT[:, k, t * P:(t + 1) * P], gatew[:, k, :],
                                         start=(k == 0), stop=(k == KD - 1))
                        ins.then_inc(bs["lg_mm"], 1)
                        pe.wait_ge(bs["lg_mm"], 1)
                        turn_ends(pe, go[0], b, arrived)

                @block.vector
                def _(dve):
                    done = [0]

                    def link(ins):
                        done[0] += 1
                        ins.then_inc(bs["dve_chain"], 1)
                        dve.wait_ge(bs["dve_chain"], done[0])

                    dve.wait_ge(for_ffn, 16 * 3)
                    dve.wait_ge(for_cst, 48)
                    dve.wait_ge(prep_pool, 3)
                    link(dve.memset(wsc[:, :], 0.0))
                    ws = (wgu_f[0], wgu_f[1], wdn_f)
                    for n, w in enumerate(ws):
                        ins = dve.tensor_reduce(wsc[:, n:n + 1], w, AX.X, ALU.add, apply_absolute_value=True)
                    ins.then_inc(prep, 1)
                    dve.tensor_copy(identb[:, :], ident)
                    dve.tensor_copy(maskb[:, :], fh[:, 0:M_END])
                    dve.tensor_copy(trib[:, :], cst[:, C_TRI:C_TRI + 2 * P])
                    dve.wait_ge(prep_pe, 1)
                    link(dve.tensor_scalar(wsc[:, 4:8], bank(7)[:, 0:4], 1.0 / (I0 * D), EPS_Q, ALU.mult, ALU.max))
                    link(dve.reciprocal(wsc[:, 8:12], wsc[:, 4:8]))
                    for n, w in enumerate(ws):
                        q = qgu[:, :, n * I0:(n + 1) * I0] if n < 2 else qdn[:, :, :]
                        link(dve.tensor_scalar(w, w, wsc[:, 8 + n:9 + n], MAGIC, ALU.mult, ALU.add))
                        link(dve.tensor_scalar(w, w, MAGIC + 1.0, MAGIC - 1.0, ALU.min, ALU.max))
                        link(dve.tensor_scalar(q, w.rearrange("p (k n) -> p k n", k=q.shape[1]), MAGIC, None,
                                               ALU.subtract))
                    link(dve.tensor_tensor(wsc[:, 12:13], wsc[:, 4:5], wsc[:, 4:5], ALU.mult))
                    link(dve.tensor_tensor(wsc[:, 12:13], wsc[:, 12:13], wsc[:, 5:6], ALU.mult))
                    link(dve.tensor_scalar(wsc[:, 13:14], wsc[:, 6:7], 1.0 / 127.0, None, ALU.mult))
                    dve.wait_ge(for_attn, 16 * 8)
                    for l in range(2):
                        ab_q = ab[l][:, :].rearrange("p (b c) -> p b c", c=2)[:, :, 0:1]
                        link(dve.tensor_scalar(ab_q, ab_q, DH ** -0.5, None, ALU.mult))
                    link(dve.memset(ks[KS:KM, :, :], 1.0))
                    dve.nop().then_inc(prep, 1)
                    dve.sem_clear(bs["dve_chain"])
                    done[0] = 0

                    def ln_sum(n, t, psum, res_in, scale=None):
                        o = lnx[:, t, :]
                        if scale is None:
                            ins = dve.tensor_tensor(o, psum, res_in, ALU.add)
                        else:
                            ins = dve.scalar_tensor_tensor(o, psum, scale, res_in, ALU.mult, ALU.add)
                        ins.then_inc(bs[f"lns_done{n}"], 1)
                        dve.wait_ge(bs[f"lns_done{n}"], t + 1)
                        link(dve.bn_stats(stat[:, t % 2, :], o))
                        link(dve.bn_aggr(mv[:, t, :], stat[:, t % 2, :]))
                        dve.tensor_scalar(mv[:, t, 1:2], mv[:, t, 1:2], EPS_LN, None,
                                          ALU.add).then_inc(bs[f"var_done{n}"], 1)

                    def ln_out(n, t):
                        dve.wait_ge(bs[f"rstd_done{n}"], t + 1)
                        dve.tensor_scalar(h[:, t, :], lnx[:, t, :], mv[:, t, 0:1], rstd[:, t, 0:1], ALU.subtract,
                                          ALU.mult).then_inc(bs[f"ln_done{n}"], 1)

                    def attention(kind, l):
                        def remainders(blk):
                            for i in range(2 * blk, 2 * blk + 2):
                                dve.wait_ge(bs[f"p1_done{l}"], i + 1)
                                dve.tensor_tensor(proj[:, i % 2, :], proj[:, i % 2, :], parts[:, i, 0, :],
                                                  ALU.subtract).then_inc(bs[f"rest_done{l}"], 1)
                            for i in range(2 * blk, 2 * blk + 2):
                                dve.wait_ge(bs[f"p2_done{l}"], i + 1)
                                dve.tensor_tensor(parts[:, i, 2, :], proj[:, i % 2, :], parts[:, i, 1, :],
                                                  ALU.subtract).then_inc(bs[f"part_done{l}"], 1)

                        remainders(0)
                        for t in range(NT):
                            dve.wait_ge(bs[f"v_mm{l}"], t + 1)
                            dve.tensor_tensor(vaug[:, t, :].rearrange("p (h s) -> p h s", s=SLOT)[:, :, 0:DH],
                                              bank(4 + t % 2)[:, 0:D].rearrange("p (h s) -> p h s", s=DH),
                                              ar[l][:, 0:D].rearrange("p (h s) -> p h s", s=DH),
                                              ALU.add).then_inc(bs[f"v_done{l}"], 1)
                        remainders(1)
                        for g in range(NG):
                            for t in range(NT):
                                lo, hi = k_range(kind, t)
                                if kind == CAUSAL:
                                    mask = maskb[:, M_CAUSAL + S - (hi - lo):M_CAUSAL + S]
                                else:
                                    c = M_WINDOW + lo - (t * P - HALF_WINDOW)
                                    mask = maskb[:, c:c + hi - lo]
                                for j in range(HG):
                                    i = g * NT * HG + t * HG + j
                                    dve.wait_ge(bs[f"s_mm{l}"], i + 1)
                                    dve.tensor_tensor_reduce(
                                        out=junk[:, j % 2, 0:hi - lo], in0=bank(4 + j % 2)[:, 0:hi - lo], in1=mask,
                                        scale=-1.0, scalar=3.0e38, op0=ALU.add, op1=ALU.min,
                                        accum_out=nmax[:, g % 2, j, t:t + 1]
                                    ).then_inc(bs[f"max_done{l}"], 1)
                            split_maxima(l, g)
                        for t in range(NT):
                            heads = bank(4 + t % 2).rearrange("p (h s) -> p h s", s=SLOT)
                            dve.wait_ge(bs[f"ob_mm{l}"], t + 1)
                            link(dve.reciprocal(rsum[:, t, :].rearrange("p (h o) -> p h o", o=1),
                                                heads[:, :, DH:DH + 1]))
                            dve.tensor_tensor(att[:, t, :].rearrange("p (h s) -> p h s", s=DH), heads[:, :, 0:DH],
                                              rsum[:, t, :].rearrange("p (h o) -> p h o", o=1).to_broadcast(
                                                  [P, H, DH]), ALU.mult).then_inc(bs[f"o_done{l}"], 1)
                        dve.wait_ge(bs[f"res_done{l}"], NT)
                        for t in range(NT + 1):
                            if t < NT:
                                dve.wait_ge(bs[f"pr_mm{l}"], t + 1)
                                ln_sum(2 * l, t, bank(t % 2)[:, 0:D], res[:, t, :])
                            if t:
                                ln_out(2 * l, t - 1)

                    def split_maxima(l, g):
                        dve.wait_ge(bs[f"max_done{l}"], NT * HG * (g + 1))
                        full = nmax[:, g % 2, :, :]
                        dst = nparts[:, g % 2, :, :].rearrange("p t (c j) -> p j t c", c=3)
                        if g >= 2:
                            dve.wait_ge(bs[f"nm_mm{l}"], g - 1)
                        link(dve.tensor_copy(dst[:, :, :, 0], full))
                        link(dve.tensor_tensor(nrest[:, :, :], full, dst[:, :, :, 0], ALU.subtract))
                        link(dve.tensor_copy(dst[:, :, :, 1], nrest[:, :, :]))
                        dve.tensor_tensor(dst[:, :, :, 2], nrest[:, :, :], dst[:, :, :, 1],
                                          ALU.subtract).then_inc(bs[f"nparts_done{l}"], 1)

                    def quant(t):
                        c = small[:, 8 * (t % 4):8 * (t % 4) + 8]
                        dve.wait_ge(bs["ln_done0"], t + 1)
                        link(dve.tensor_reduce(c[:, 0:1], h[:, t, :], AX.X, ALU.max, apply_absolute_value=True))
                        link(dve.tensor_scalar(c[:, 0:1], c[:, 0:1], EPS_Q, 1.0 / 127.0, ALU.max, ALU.mult))
                        link(dve.reciprocal(c[:, 1:2], c[:, 0:1]))
                        link(dve.tensor_scalar(fq[:, :], h[:, t, :], c[:, 1:2], MAGIC, ALU.mult, ALU.add))
                        if t >= 2:
                            dve.wait_ge(bs["fq_mm"], t - 1)
                        dve.tensor_scalar(fqb[:, t % 2, :], fq[:, :], MAGIC, 127.0, ALU.subtract,
                                          ALU.min).then_inc(bs["fq_done"], 1)
                        link(dve.tensor_tensor(c[:, 2:3], c[:, 0:1], c[:, 0:1], ALU.mult))
                        link(dve.tensor_tensor(c[:, 2:3], c[:, 2:3], c[:, 0:1], ALU.mult))
                        link(dve.tensor_tensor(c[:, 2:3], c[:, 2:3], wsc[:, 12:13], ALU.mult))

                    def hidden(t):
                        c = small[:, 8 * (t % 4):8 * (t % 4) + 8]
                        dve.wait_ge(bs["fsq_done"], t + 1)
                        dve.tensor_tensor(fh[:, :].rearrange("p (a n) -> p a n", a=2),
                                          hid[:, 2:4, :], ps[:, 2:4, :],
                                          ALU.mult).then_inc(bs["fh_done"], 1)
                        dve.wait_ge(bs["fh_done"], t + 1)
                        link(dve.tensor_reduce(c[:, 3:4], fh[:, :], AX.X, ALU.max, apply_absolute_value=True))
                        link(dve.tensor_tensor(c[:, 3:4], c[:, 3:4], c[:, 2:3], ALU.mult))
                        link(dve.tensor_scalar(c[:, 3:4], c[:, 3:4], EPS_Q, None, ALU.max))
                        link(dve.reciprocal(c[:, 4:5], c[:, 3:4]))
                        link(dve.tensor_tensor(c[:, 4:5], c[:, 4:5], c[:, 2:3], ALU.mult))
                        link(dve.tensor_scalar(c[:, 4:5], c[:, 4:5], 127.0, None, ALU.mult))
                        link(dve.tensor_tensor(c[:, 5:6], c[:, 3:4], wsc[:, 13:14], ALU.mult))
                        link(dve.tensor_scalar(fh[:, :], fh[:, :], c[:, 4:5], MAGIC, ALU.mult, ALU.add))
                        if t:
                            dve.wait_ge(bs["fq2_mm"], t)
                        dve.tensor_scalar(fq2[:, :], fh[:, :], MAGIC, 127.0, ALU.subtract,
                                          ALU.min).then_inc(bs["fq2_done"], 1)

                    with dve.Fori(0, B) as b:
                        for m in range(ME):
                            dve.wait_ge(bs["relu_done"], m + 1)
                            dve.tensor_tensor(hid[:, m, :], bank(2 * (m % 2) + 1), relu_g[:, m % 2, :],
                                              ALU.mult).then_inc(bs["hid_done"], 1)
                        for t in range(NT):
                            dve.wait_ge(bs["h0_mm"], t + 1)
                            dve.tensor_copy(h[:, t, :], bank(4 + t % 2)[:, 0:D]).then_inc(bs["h0_done"], 1)
                        dve.wait_ge(for_attn, 16 * 8)
                        attention(WINDOW, 0)
                        quant(0)
                        quant(1)
                        hidden(0)
                        for t in range(NT):
                            if t + 2 < NT:
                                quant(t + 2)
                            if t + 1 < NT:
                                hidden(t + 1)
                            dve.wait_ge(bs["fdn_mm"], t + 1)
                            ln_sum(1, t, bank(5)[:, 0:D], h[:, t, :], scale=small[:, 8 * t + 5:8 * t + 6])
                            ln_out(1, t)
                        attention(CAUSAL, 1)
                        dve.wait_ge(bs["lg_mm"], 1)
                        dve.tensor_copy(logits[:, bass.ds(b * NT, NT), :],
                                        bank(4)[:, 0:NT * E].rearrange("p (t e) -> p t e", e=E)
                                        ).then_inc(bs["lg_done"], 1)
                        dve.wait_ge(bs["lg_done"], 1)
                        turn_ends(dve, go[0], b, arrived)
                        done[0] = 0

        with ExitStack() as c3:
            def sb3(name, shape, dt=F32):
                return c3.enter_context(nc.sbuf_tensor(name, shape, dt))

            R = {n: sb3(f"r_{n}", [P, NTT, E]) for n in ("e", "p", "q", "m0", "m1", "t0")}
            rc = sb3("rc", [P, 8, NTT])
            mk = sb3("mk", [P, 2, E, NTT], BF16)
            mkf = sb3("mkf", [P, 2, E, NTT])
            tot = sb3("tot", [P, 2, 2, E, NTT])
            exc = sb3("exc", [P, 2, E, NTT])
            loc = sb3("loc", [P, 2, NTT])
            idx = sb3("idx", [P, 2, NTT])
            keep = sb3("keep", [P, 2, NTT])
            gates = sb3("gates", [P, 2, NTT])
            posu = sb3("posu", [P, 2, NTT], U32)
            w1s = sb3("w1s", [P, 2, KD, HE])
            w2s = sb3("w2s", [P, 2, MH, D])
            b1s = sb3("b1s", [P, E, MH])
            b2s = sb3("b2s", [P, 2, D])
            lnr = sb3("lnr", [P, 2 * D])
            dx = sb3("dx", [P, 2, CT, D])
            dxT = sb3("dxT", [P, 2, KD, CAP])
            hTe = sb3("hTe", [P, MH, CAP])
            ysb = sb3("ysb", [P, CT, D])
            dx_v = disp.rearrange("(e t p) d -> e p t d", p=P, t=CT)
            y_v = ydram[0:ROWS, :].rearrange("(e t p) d -> e p t d", p=P, t=CT)

            with nc.Block() as block:
                def load_weights(eng, e, s, sem_):
                    eng.dma_start(w1s[:, s, :, :], w1[bass.ds(e, 1), :, :, :].rearrange("o p k n -> p (o k) n")
                                  ).then_inc(sem_, 16)
                    eng.dma_start(w2s[:, s, :, :], w2[bass.ds(e, 1), :, :, :].rearrange("o p k n -> p (o k) n")
                                  ).then_inc(sem_, 16)
                    eng.dma_start(b2s[:, s, :], b2[bass.ds(e, 1), :, :].rearrange("o p n -> p (o n)")
                                  ).then_inc(sem_, 16)

                def load_rows(eng, e, s, sem_):
                    eng.dma_start(dx[:, s, :, :], dx_v[bass.ds(e, 1), :, :, :].rearrange("o p t d -> p (o t) d")
                                  ).then_inc(sem_, 16)

                @block.sync
                def _(sp):
                    sp.dma_start(b1s[:, :, :], b1).then_inc(wa_in, 16)
                    sp.dma_start(lnr[:, :], lnrow).then_inc(wa_in, 16)
                    load_weights(sp, 0, 0, wa_in)
                    sp.wait_ge(scattered, 16 * 2 * NTT)
                    load_rows(sp, 0, 0, wa_in)
                    with sp.Fori(0, E // 2) as i:
                        load_weights(sp, i * 2 + 1, 1, es["wb_in"])
                        load_rows(sp, i * 2 + 1, 1, es["wb_in"])
                        nxt = (i * 2 + 2) % E
                        sp.wait_ge(es["f2_mm"], CT)
                        sp.wait_ge(es["y_done"], CT)
                        load_weights(sp, nxt, 0, es["wa_next"])
                        load_rows(sp, nxt, 0, es["wa_next"])
                        for j in range(2):
                            sp.wait_ge(es["y_done"], CT * (j + 1))
                            sp.dma_start(y_v[bass.ds(i * 2 + j, 1), :, :, :].rearrange("o p t d -> p (o t) d"),
                                         ysb[:, :, :]).then_inc(es["y_out"], 16)
                        sp.wait_ge(es["y_out"], 32)
                        sp.wait_ge(es["wa_next"], 64)
                        turn_ends(sp, go[1], i, e_arrived, clear=expert_range)

                @block.gpsimd
                def _(pool):
                    pool.wait_ge(routed, 1)
                    for t in range(NTT):
                        for k in range(2):
                            pool.indirect_dma_start(
                                out=disp, out_offset=bass.IndirectOffsetOnAxis(ap=posu[:, k, t:t + 1], axis=0),
                                in_=h3[:, t, :], in_offset=None, bounds_check=ROWS - 1,
                                oob_is_err=False).then_inc(scattered, 16)
                    with pool.Fori(0, E // 2) as i:
                        turn_ends(pool, go[1], i, e_arrived)

                @block.tensor
                def _(pe):
                    mm = pe.matmul
                    pe.wait_ge(route_pe, 1)
                    mf = mk[:, :, :, :].rearrange("p a b c -> p (a b c)")
                    mm(bank(0)[:, 0:2 * E * NTT], trib[:, 0:P], mf, start=True, stop=True)
                    mm(bank(1)[:, 0:2 * E * NTT], trib[:, P:2 * P], mf, start=True, stop=True).then_inc(route_pe, 1)
                    pe.wait_ge(wa_in, 16 * 6)

                    def turn_rows(s):
                        for t in range(CT):
                            n = s * CT + t
                            if n >= 2:
                                pe.wait_ge(es["xT_done"], n - 1)
                            for k in range(KD):
                                ins = pe.transpose(bank(6 + n % 2)[:, k * P:(k + 1) * P],
                                                   dx[:, s, t, k * P:(k + 1) * P], ident)
                            ins.then_inc(es["xT_mm"], 1)

                    def fc1(s):
                        pe.wait_ge(es["xT_done"], CT * (s + 1))
                        for m in range(MH):
                            n = s * MH + m
                            if n >= 2:
                                pe.wait_ge(es["silu_done"], n - 1)
                            for c in range(2):
                                for k in range(KD):
                                    ins = mm(bank(2 * (n % 2) + c)[:, 0:HC], w1s[:, s, k, m * P:(m + 1) * P],
                                             dxT[:, s, k, c * HC:(c + 1) * HC], start=(k == 0), stop=(k == KD - 1))
                            ins.then_inc(es["f1_mm"], 1)

                    def fc2(s):
                        pe.wait_ge(es["silu_done"], MH * (s + 1))
                        for t in range(CT):
                            n = s * CT + t
                            if n >= 2:
                                pe.wait_ge(es["y_done"], n - 1)
                            for m in range(MH):
                                ins = mm(bank(4 + n % 2)[:, 0:D], hTe[:, m, t * P:(t + 1) * P], w2s[:, s, m, :],
                                         start=(m == 0), stop=(m == MH - 1))
                            ins.then_inc(es["f2_mm"], 1)

                    with pe.Fori(0, E // 2) as i:
                        turn_rows(0)
                        fc1(0)
                        pe.wait_ge(es["wb_in"], 64)
                        turn_rows(1)
                        fc2(0)
                        fc1(1)
                        fc2(1)
                        pe.wait_ge(es["f2_mm"], 2 * CT)
                        turn_ends(pe, go[1], i, e_arrived)

                @block.scalar
                def _(act):
                    act.wait_ge(route_act, 1)
                    act.activation(R["e"][:, :, :], R["t0"][:, :, :], ACT.Exp).then_inc(route_act, 1)
                    act.wait_ge(wa_in, 16 * 6)
                    with act.Fori(0, E // 2) as i:
                        for s in range(2):
                            for m in range(MH):
                                n = s * MH + m
                                act.wait_ge(es["f1_mm"], n + 1)
                                if m == 0 and s:
                                    act.wait_ge(es["f2_mm"], CT)
                                act.activation(hTe[:, m, :].rearrange("p (a n) -> p a n", a=2),
                                               ps[:, 2 * (n % 2):2 * (n % 2) + 2, 0:HC], ACT.Silu,
                                               bias=b1s[:, bass.ds(i * 2 + s, 1), m:m + 1].rearrange(
                                                   "p a b -> p (a b)")).then_inc(es["silu_done"], 1)
                        act.wait_ge(es["silu_done"], 2 * MH)
                        turn_ends(act, go[1], i, e_arrived)

                @block.vector
                def _(dve):
                    done = [0]

                    def link(ins):
                        done[0] += 1
                        ins.then_inc(dve_route, 1)
                        dve.wait_ge(dve_route, done[0])

                    def bc(v):
                        return v.rearrange("p (t o) -> p t o", o=1).to_broadcast([P, NTT, E])

                    link(dve.tensor_reduce(rc[:, 0, :], logits[:, :, :], AX.X, ALU.max))
                    dve.tensor_tensor(R["t0"][:, :, :], logits[:, :, :], bc(rc[:, 0, :]),
                                      ALU.subtract).then_inc(route_act, 1)
                    dve.wait_ge(route_act, 2)
                    link(dve.tensor_reduce(rc[:, 1, :], R["e"][:, :, :], AX.X, ALU.add))
                    link(dve.reciprocal(rc[:, 2, :], rc[:, 1, :]))
                    link(dve.tensor_tensor(R["p"][:, :, :], R["e"][:, :, :], bc(rc[:, 2, :]), ALU.mult))
                    rev = cst[:, C_REV:C_REV + P].rearrange("p (t e) -> p t e", e=E)
                    ind = cst[:, C_IDX:C_IDX + P].rearrange("p (t e) -> p t e", e=E)
                    cur = R["p"]
                    for k in range(2):
                        link(dve.tensor_reduce(rc[:, 3 + k, :], cur[:, :, :], AX.X, ALU.max))
                        link(dve.tensor_tensor(R["t0"][:, :, :], cur[:, :, :], bc(rc[:, 3 + k, :]), ALU.is_equal))
                        link(dve.tensor_tensor(R["t0"][:, :, :], R["t0"][:, :, :], rev, ALU.mult))
                        link(dve.tensor_reduce(rc[:, 5, :], R["t0"][:, :, :], AX.X, ALU.max))
                        m = R[f"m{k}"]
                        link(dve.tensor_tensor(m[:, :, :], R["t0"][:, :, :], bc(rc[:, 5, :]), ALU.is_equal))
                        link(dve.tensor_copy(mk[:, k, :, :], m[:, :, :].rearrange("p t e -> p e t")))
                        link(dve.tensor_copy(mkf[:, k, :, :], m[:, :, :].rearrange("p t e -> p e t")))
                        link(dve.tensor_tensor(R["t0"][:, :, :], m[:, :, :], ind, ALU.mult))
                        link(dve.tensor_reduce(idx[:, k, :], R["t0"][:, :, :], AX.X, ALU.add))
                        if k == 0:
                            link(dve.tensor_scalar(R["t0"][:, :, :], m[:, :, :], -4.0, None, ALU.mult))
                            link(dve.tensor_tensor(R["q"][:, :, :], cur[:, :, :], R["t0"][:, :, :], ALU.add))
                            cur = R["q"]
                    dve.nop().then_inc(route_pe, 1)
                    link(dve.tensor_tensor(rc[:, 5, :], rc[:, 3, :], rc[:, 4, :], ALU.add))
                    link(dve.tensor_scalar(rc[:, 5, :], rc[:, 5, :], EPS_GATE, None, ALU.max))
                    link(dve.reciprocal(rc[:, 6, :], rc[:, 5, :]))
                    for k in range(2):
                        link(dve.tensor_tensor(gates[:, k, :], rc[:, 3 + k, :], rc[:, 6, :], ALU.mult))
                    dve.wait_ge(route_pe, 2)
                    flat = "p a b c -> p (a b) c"
                    first = bank(1)[:, 0:2 * E * NTT].rearrange("p (a b c) -> p a b c", a=2, b=E)
                    before = bank(0)[:, 0:2 * E * NTT].rearrange("p (a b c) -> p a b c", a=2, b=E)
                    link(dve.tensor_copy(tot[:, 0, :, :, :], first))
                    a = 0
                    step = 1
                    while step < NTT:
                        src = tot[:, a, :, :, :].rearrange(flat)
                        dst = tot[:, 1 - a, :, :, :].rearrange(flat)
                        dve.tensor_copy(dst[:, :, 0:step], src[:, :, 0:step])
                        link(dve.tensor_tensor(dst[:, :, step:], src[:, :, step:], src[:, :, 0:NTT - step], ALU.add))
                        a = 1 - a
                        step *= 2
                    link(dve.tensor_tensor(exc[:, :, :, :], tot[:, a, :, :, :], first, ALU.subtract))
                    link(dve.tensor_tensor(exc[:, 1, :, :], exc[:, 1, :, :],
                                           tot[:, a, 0, :, NTT - 1:NTT].to_broadcast([P, E, NTT]), ALU.add))
                    link(dve.tensor_tensor(exc[:, :, :, :], exc[:, :, :, :], before, ALU.add))
                    link(dve.tensor_tensor(exc[:, :, :, :], exc[:, :, :, :], mkf[:, :, :, :], ALU.mult))
                    for k in range(2):
                        link(dve.tensor_reduce(loc[:, k, :], exc[:, k, :, :].rearrange("p e t -> p t e"), AX.X,
                                               ALU.add))
                    link(dve.tensor_scalar(keep[:, :, :], loc[:, :, :], float(CAP), None, ALU.is_lt))
                    link(dve.tensor_tensor(gates[:, :, :], gates[:, :, :], keep[:, :, :], ALU.mult))
                    link(dve.tensor_scalar(idx[:, :, :], idx[:, :, :], float(CAP), float(-ROWS), ALU.mult, ALU.add))
                    link(dve.tensor_tensor(idx[:, :, :], idx[:, :, :], loc[:, :, :], ALU.add))
                    link(dve.tensor_tensor(idx[:, :, :], idx[:, :, :], keep[:, :, :], ALU.mult))
                    link(dve.tensor_scalar(idx[:, :, :], idx[:, :, :], float(ROWS), None, ALU.add))
                    dve.tensor_copy(posu[:, :, :], idx[:, :, :]).then_inc(routed, 1)
                    dve.wait_ge(wa_in, 16 * 6)
                    with dve.Fori(0, E // 2) as i:
                        def evac_rows(s):
                            for t in range(CT):
                                n = s * CT + t
                                dve.wait_ge(es["xT_mm"], n + 1)
                                dve.tensor_copy(dxT[:, s, :, t * P:(t + 1) * P],
                                                bank(6 + n % 2)[:, 0:KD * P].rearrange("p (k n) -> p k n", k=KD)
                                                ).then_inc(es["xT_done"], 1)

                        def evac_out(s):
                            for t in range(CT):
                                n = s * CT + t
                                dve.wait_ge(es["f2_mm"], n + 1)
                                if t == 0 and s:
                                    dve.wait_ge(es["y_out"], 16)
                                dve.tensor_tensor(ysb[:, t, :], bank(4 + n % 2)[:, 0:D], b2s[:, s, :],
                                                  ALU.add).then_inc(es["y_done"], 1)

                        evac_rows(0)
                        dve.wait_ge(es["wb_in"], 64)
                        evac_rows(1)
                        evac_out(0)
                        evac_out(1)
                        dve.wait_ge(es["y_done"], 2 * CT)
                        turn_ends(dve, go[1], i, e_arrived)

            yk = w1s[:, :, :, :].rearrange("p a b c -> p (a b c)")
            y_at = [yk.rearrange("p (t d) -> p t d", d=D), w2s[:, :, :, :].rearrange("p a b d -> p (a b) d")]
            xa = dx[:, 0, :, :]
            xb = dx[:, 1, :, :]
            n1 = hTe[:, :, :].rearrange("p m n -> p (m n)")[:, 0:NT * D].rearrange("p (t d) -> p t d", d=D)
            n2 = hTe[:, :, :].rearrange("p m n -> p (m n)")[:, NT * D:2 * NT * D].rearrange("p (t d) -> p t d", d=D)
            outv = out.rearrange("b (t p) d -> b p t d", p=P)
            with nc.Block() as block:
                @block.sync
                def _(sp):
                    with sp.Fori(0, B) as b:
                        sp.wait_ge(cs["fin_done"], NT)
                        sp.dma_start(outv[bass.ds(b, 1), :, :, :].rearrange("o p t d -> p (o t) d"),
                                     n2).then_inc(cs["out_done"], 16)
                        sp.wait_ge(cs["out_done"], 16)
                        turn_ends(sp, go[2], b, c_arrived, clear=combine_range)

                @block.gpsimd
                def _(pool):
                    for t in range(NTT):
                        for k in range(2):
                            pool.indirect_dma_start(
                                out=y_at[k][:, t, :], out_offset=None, in_=ydram,
                                in_offset=bass.IndirectOffsetOnAxis(ap=posu[:, k, t:t + 1], axis=0)
                            ).then_inc(gathered, 16)
                    with pool.Fori(0, B) as b:
                        for t in range(2 * NT):
                            pool.wait_ge(cs["cvar_done"], t + 1)
                            pool.tensor_tensor(rstd[:, t, 0:1], mv[:, t, 1:2], neg_half[:, 0:1],
                                               ALU.pow).then_inc(cs["crstd_done"], 1)
                        pool.wait_ge(cs["crstd_done"], 2 * NT)
                        turn_ends(pool, go[2], b, c_arrived)

                @block.scalar
                def _(act):
                    with act.Fori(0, B) as b:
                        turn_ends(act, go[2], b, c_arrived)

                @block.tensor
                def _(pe):
                    with pe.Fori(0, B) as b:
                        turn_ends(pe, go[2], b, c_arrived)

                @block.vector
                def _(dve):
                    dve.wait_ge(gathered, 16 * 2 * NTT)
                    done = [0]

                    def link(ins):
                        done[0] += 1
                        ins.then_inc(cs["c_chain"], 1)
                        dve.wait_ge(cs["c_chain"], done[0])

                    def moments(n, x):
                        link(dve.bn_stats(stat[:, n % 2, :], x))
                        link(dve.bn_aggr(mv[:, n, :], stat[:, n % 2, :]))
                        dve.tensor_scalar(mv[:, n, 1:2], mv[:, n, 1:2], EPS_LN, None,
                                          ALU.add).then_inc(cs["cvar_done"], 1)

                    with dve.Fori(0, B) as b:
                        def tile(v, t):
                            return v[:, bass.ds(b * NT + t, 1), :].rearrange("p o d -> p (o d)")

                        for t in range(NT):
                            g = [gates[:, k, bass.ds(b * NT + t, 1)] for k in range(2)]
                            link(dve.tensor_scalar(xa[:, t, :], tile(y_at[0], t), g[0], None, ALU.mult))
                            link(dve.scalar_tensor_tensor(xa[:, t, :], tile(y_at[1], t), g[1], xa[:, t, :], ALU.mult,
                                                          ALU.add))
                            link(dve.tensor_tensor(xa[:, t, :], xa[:, t, :], tile(h3, t), ALU.add))
                            moments(t, xa[:, t, :])
                        for t in range(NT):
                            dve.wait_ge(cs["crstd_done"], t + 1)
                            link(dve.tensor_scalar(n1[:, t, :], xa[:, t, :], mv[:, t, 0:1], rstd[:, t, 0:1],
                                                   ALU.subtract, ALU.mult))
                            link(dve.tensor_tensor(n1[:, t, :], n1[:, t, :], lnr[:, 0:D], ALU.mult))
                            link(dve.tensor_tensor(n1[:, t, :], n1[:, t, :], lnr[:, D:2 * D], ALU.add))
                            link(dve.tensor_tensor(xb[:, t, :], n1[:, t, :], tile(h3, t), ALU.add))
                            moments(NT + t, xb[:, t, :])
                        for t in range(NT):
                            dve.wait_ge(cs["crstd_done"], NT + t + 1)
                            dve.tensor_scalar(n2[:, t, :], xb[:, t, :], mv[:, NT + t, 0:1], rstd[:, NT + t, 0:1],
                                              ALU.subtract, ALU.mult).then_inc(cs["fin_done"], 1)
                        dve.wait_ge(cs["fin_done"], NT)
                        turn_ends(dve, go[2], b, c_arrived)
                        done[0] = 0


def kernel(**inputs):
    import concourse.bacc as _bacc
    from concourse.bass_utils import run_bass_kernel_spmd as _run

    a = {k: np.asarray(v) for k, v in inputs.items()}

    def rows(w):
        return w.reshape(-1, P, w.shape[1]).transpose(1, 0, 2)

    def wide(*vs):
        return np.broadcast_to(np.concatenate(vs)[None], (P, sum(v.size for v in vs)))

    def by_dim(w):
        return w.reshape(-1, NB, HB, DH).swapaxes(2, 3).reshape(w.shape)

    wattn, wo, battn, brow = [], [], [], []
    for l in range(2):
        w = {n: (a[f"L{l}_attn_W{n}"] if l == 0 else a[f"L{l}_attn_W{n}"].T) for n in "qkvo"}
        bias = {n: a[f"L{l}_attn_b{n}"] for n in "qkvo"}
        wattn.append(rows(np.concatenate([by_dim(w["q"]), by_dim(w["k"]), w["v"]], axis=1)))
        wo.append(rows(w["o"]))
        battn.append(np.stack([by_dim(bias[n]).reshape(NB, P) for n in "qk"], axis=1).reshape(2 * NB, P).T)
        brow.append(wide(bias["v"], bias["o"]))

    p = np.arange(P)[:, None]
    c = np.arange(S)[None, :]
    consts = np.zeros((P, C_END), np.float32)
    consts[:, C_ID:C_ID + P] = np.eye(P)
    masks = np.zeros((P, M_END), np.float32)
    masks[:, M_CAUSAL:M_CAUSAL + S] = np.where(c - (S - P) > p, MASKED, 0.0)
    w = np.arange(2 * P)[None, :] - HALF_WINDOW
    masks[:, M_WINDOW:M_WINDOW + 2 * P] = np.where(np.abs(w - p) > HALF_WINDOW, MASKED, 0.0)
    consts[:, C_TRI:C_TRI + P] = p < np.arange(P)[None, :]
    consts[:, C_ONE:C_ONE + P] = 1.0
    consts[:, C_REV:C_REV + P] = E - np.arange(P)[None, :] % E
    consts[:, C_IDX:C_IDX + P] = np.arange(P)[None, :] % E

    ins = {
        "xT": a["x"].transpose(3, 2, 0, 1).reshape(4, D, N),
        "w01": rows(np.concatenate([a["L0_tok_W0"].T, a["L0_tok_W1"].T], axis=1)),
        "wtok": rows(a["L0_tok_Wo"].T),
        "wattn": np.stack(wattn), "wo": np.stack(wo), "battn": np.stack(battn), "brow": np.stack(brow),
        "wq0": np.stack([rows(a["L0_ffn_w_gate"].T).reshape(P, -1), rows(a["L0_ffn_w_up"].T).reshape(P, -1)]),
        "wdn": rows(a["L0_ffn_w_down"].T).reshape(P, -1),
        "wgate": rows(a["L1_ffn_wg"]),
        "consts": consts, "masks": masks,
        "w1": a["L1_ffn_fc1_w"].transpose(0, 2, 1).reshape(E, KD, P, HE).transpose(0, 2, 1, 3),
        "w2": a["L1_ffn_fc2_w"].reshape(E, MH, P, D).transpose(0, 2, 1, 3),
        "b1": a["L1_ffn_fc1_b"].reshape(E, MH, P).transpose(2, 0, 1),
        "b2": np.broadcast_to(a["L1_ffn_fc2_b"][:, None, :], (E, P, D)),
        "lnrow": wide(a["L1_ffn_ln_gamma"], a["L1_ffn_ln_beta"]),
    }
    ins = {n: np.ascontiguousarray(v) for n, v in ins.items()}
    nc = _bacc.Bacc("TRN2", target_bir_lowering=False, num_devices=1)
    aps = [nc.dram_tensor(n, v.shape, mybir.dt.from_np(v.dtype), kind="ExternalInput").ap() for n, v in ins.items()]
    out = nc.dram_tensor("out", (B, S, D), F32, kind="ExternalOutput").ap()
    build(nc, *aps, out)
    return _run(nc, [ins], core_ids=[0]).results[0]["out"]
```
